# Optimizing a Trainium2 kernel written in Bass

```python
import numpy as np
import jax
import jax.numpy as jnp

def _softmax(x, axis=-1):
    return jax.nn.softmax(x, axis=axis)

def _gelu(x):
    return jax.nn.gelu(x, approximate=True)

def _silu(x):
    return jax.nn.silu(x)

def _sigmoid(x):
    return jax.nn.sigmoid(x)

def _layernorm(x, axis=-1, eps=1e-05):
    m = jnp.mean(x, axis=axis, keepdims=True)
    v = jnp.var(x, axis=axis, keepdims=True)
    return (x - m) / jnp.sqrt(v + eps)

def _scatter_add(tgt, idx, src, axis=0):
    return tgt.at[idx].add(src)

def _segment_sum(src, seg, n):
    return jax.ops.segment_sum(src, seg, n)
kernel_name = 'mk_adj_preln_d4_adj_r2_4861ee'

def setup_inputs(seed: int=0):
    np.random.seed(seed)
    _w = jnp.asarray

    def _rec_inputs():
        import jax
        import jax.numpy as jnp
        _gk = jax.random.key(seed)
        x = -0.000929 + 1 * jax.random.normal(jax.random.fold_in(_gk, 1), (2048, 256), jnp.float32)
        _a = jax.random.bernoulli(jax.random.fold_in(_gk, 2), 0.00390625, (2048, 2048))
        _a = jnp.logical_or(_a, jnp.swapaxes(_a, -1, -2))
        _a = jnp.logical_or(_a, jnp.eye(2048, dtype=bool))
        adj = _a.astype(jnp.int32)
        return (x, adj)
    x, adj = _rec_inputs()

    def _L0_gnn_setup():
        import jax, jax.numpy as jnp
        import numpy as np
        B, IN_F, OUT_F, H = (1024, 256, 256, 8)
        D = OUT_F // H
        key = jax.random.key(seed)
        ks = jax.random.split(key, 4)
        x = jax.random.normal(ks[0], (B, IN_F), dtype=jnp.float32)
        W_w = jax.random.normal(ks[1], (OUT_F, IN_F), dtype=jnp.float32) * (1.0 / np.sqrt(IN_F))
        W_b = jnp.zeros((OUT_F,), dtype=jnp.float32)
        a = jax.random.normal(ks[2], (2 * D, 1), dtype=jnp.float32) * 0.1
        adj = jax.random.randint(ks[3], (B, B), 0, 2, dtype=jnp.int32)
        return {'x': x, 'adj': adj, 'W_w': W_w, 'W_b': W_b, 'a': a}
    _L0_gnn_all = _L0_gnn_setup()
    _L0_gnn_in = {k: v for k, v in _L0_gnn_all.items() if k in ('W_w', 'W_b', 'a')}
    del _L0_gnn_all

    def _L1_gnn_setup():
        import jax, jax.numpy as jnp
        import numpy as np
        N, D_IN, D_OUT = (4096, 256, 256)
        key = jax.random.key(seed)
        ks = jax.random.split(key, 8)
        scale_in = 1.0 / np.sqrt(D_IN)
        scale_cat = 1.0 / np.sqrt(2 * D_OUT)
        return {'x': jax.random.normal(ks[0], (N, D_IN), dtype=jnp.float32), 'adj': jax.random.randint(ks[1], (N, N), 0, 2, dtype=jnp.int32), 'W_self': jax.random.uniform(ks[2], (D_IN, D_OUT), jnp.float32, -scale_in, scale_in), 'b_self': jax.random.uniform(ks[3], (D_OUT,), jnp.float32, -scale_in, scale_in), 'W_nb': jax.random.uniform(ks[4], (D_IN, D_OUT), jnp.float32, -scale_in, scale_in), 'b_nb': jax.random.uniform(ks[5], (D_OUT,), jnp.float32, -scale_in, scale_in), 'W_comb': jax.random.uniform(ks[6], (2 * D_OUT, D_OUT), jnp.float32, -scale_cat, scale_cat), 'b_comb': jax.random.uniform(ks[7], (D_OUT,), jnp.float32, -scale_cat, scale_cat)}
    _L1_gnn_all = _L1_gnn_setup()
    _L1_gnn_in = {k: v for k, v in _L1_gnn_all.items() if k in ('W_self', 'b_self', 'W_nb', 'b_nb', 'W_comb', 'b_comb')}
    del _L1_gnn_all

    def _L2_gnn_setup():
        import jax, jax.numpy as jnp
        import numpy as np
        key = jax.random.key(seed)
        kX, kA, k1, k2, k3, k4 = jax.random.split(key, 6)
        N, Cin, Cout = (4096, 256, 256)
        X = jax.random.normal(kX, (N, Cin), dtype=jnp.float32)
        A = jax.random.randint(kA, (N, N), 0, 2, dtype=jnp.int32)
        bound = 1.0 / np.sqrt(Cin)
        W_nb = jax.random.uniform(k1, (Cout, Cin), jnp.float32, -bound, bound)
        b_nb = jax.random.uniform(k2, (Cout,), jnp.float32, -bound, bound)
        W_line = jax.random.uniform(k3, (Cout, Cin), jnp.float32, -bound, bound)
        b_line = jax.random.uniform(k4, (Cout,), jnp.float32, -bound, bound)
        return {'X': X, 'A': A, 'W_nb': W_nb, 'b_nb': b_nb, 'W_line': W_line, 'b_line': b_line, 'neibor_num': 64}
    _L2_gnn_all = _L2_gnn_setup()
    _L2_gnn_in = {k: v for k, v in _L2_gnn_all.items() if k in ('W_nb', 'b_nb', 'W_line', 'b_line')}
    del _L2_gnn_all

    def _L3_gnn_setup():
        import jax, jax.numpy as jnp
        import numpy as np
        N = 2048
        STATE_DIM = 256
        OUTPUT_DIM = 256
        N_STEPS = 5
        W_STD = 0.02

        def _lin_params(key, out_dim, in_dim):
            W = jax.random.normal(key, (out_dim, in_dim), dtype=jnp.float32) * W_STD
            b = jnp.zeros((out_dim,), dtype=jnp.float32)
            return (W, b)
        key = jax.random.key(seed)
        ks = jax.random.split(key, 10)
        prop_state = jax.random.normal(ks[0], (N, STATE_DIM), dtype=jnp.float32)
        A = jax.random.randint(ks[1], (N, N), 0, 2, dtype=jnp.int64)
        in_W, in_b = _lin_params(ks[2], STATE_DIM, STATE_DIM)
        out_W, out_b = _lin_params(ks[3], STATE_DIM, STATE_DIM)
        r_W, r_b = _lin_params(ks[4], STATE_DIM, 3 * STATE_DIM)
        z_W, z_b = _lin_params(ks[5], STATE_DIM, 3 * STATE_DIM)
        h_W, h_b = _lin_params(ks[6], STATE_DIM, 3 * STATE_DIM)
        o1_W, o1_b = _lin_params(ks[7], STATE_DIM, STATE_DIM)
        o2_W, o2_b = _lin_params(ks[8], OUTPUT_DIM, STATE_DIM)
        return {'prop_state': prop_state, 'A': A, 'in_W': in_W, 'in_b': in_b, 'out_W': out_W, 'out_b': out_b, 'r_W': r_W, 'r_b': r_b, 'z_W': z_W, 'z_b': z_b, 'h_W': h_W, 'h_b': h_b, 'o1_W': o1_W, 'o1_b': o1_b, 'o2_W': o2_W, 'o2_b': o2_b}
    _L3_gnn_all = _L3_gnn_setup()
    _L3_gnn_in = {k: v for k, v in _L3_gnn_all.items() if k in ('in_W', 'in_b', 'out_W', 'out_b', 'r_W', 'r_b', 'z_W', 'z_b', 'h_W', 'h_b', 'o1_W', 'o1_b', 'o2_W', 'o2_b')}
    del _L3_gnn_all
    return {'x': x, 'adj': adj, 'L0_gnn_W_w': _L0_gnn_in['W_w'], 'L0_gnn_W_b': _L0_gnn_in['W_b'], 'L0_gnn_a': _L0_gnn_in['a'], 'L1_gnn_W_self': _L1_gnn_in['W_self'], 'L1_gnn_b_self': _L1_gnn_in['b_self'], 'L1_gnn_W_nb': _L1_gnn_in['W_nb'], 'L1_gnn_b_nb': _L1_gnn_in['b_nb'], 'L1_gnn_W_comb': _L1_gnn_in['W_comb'], 'L1_gnn_b_comb': _L1_gnn_in['b_comb'], 'L2_gnn_W_nb': _L2_gnn_in['W_nb'], 'L2_gnn_b_nb': _L2_gnn_in['b_nb'], 'L2_gnn_W_line': _L2_gnn_in['W_line'], 'L2_gnn_b_line': _L2_gnn_in['b_line'], 'L3_gnn_in_W': _L3_gnn_in['in_W'], 'L3_gnn_in_b': _L3_gnn_in['in_b'], 'L3_gnn_out_W': _L3_gnn_in['out_W'], 'L3_gnn_out_b': _L3_gnn_in['out_b'], 'L3_gnn_r_W': _L3_gnn_in['r_W'], 'L3_gnn_r_b': _L3_gnn_in['r_b'], 'L3_gnn_z_W': _L3_gnn_in['z_W'], 'L3_gnn_z_b': _L3_gnn_in['z_b'], 'L3_gnn_h_W': _L3_gnn_in['h_W'], 'L3_gnn_h_b': _L3_gnn_in['h_b'], 'L3_gnn_o1_W': _L3_gnn_in['o1_W'], 'L3_gnn_o1_b': _L3_gnn_in['o1_b'], 'L3_gnn_o2_W': _L3_gnn_in['o2_W'], 'L3_gnn_o2_b': _L3_gnn_in['o2_b']}

def reference(x, adj, L0_gnn_W_w, L0_gnn_W_b, L0_gnn_a, L1_gnn_W_self, L1_gnn_b_self, L1_gnn_W_nb, L1_gnn_b_nb, L1_gnn_W_comb, L1_gnn_b_comb, L2_gnn_W_nb, L2_gnn_b_nb, L2_gnn_W_line, L2_gnn_b_line, L3_gnn_in_W, L3_gnn_in_b, L3_gnn_out_W, L3_gnn_out_b, L3_gnn_r_W, L3_gnn_r_b, L3_gnn_z_W, L3_gnn_z_b, L3_gnn_h_W, L3_gnn_h_b, L3_gnn_o1_W, L3_gnn_o1_b, L3_gnn_o2_W, L3_gnn_o2_b):
    import jax
    import jax.numpy as jnp

    def _L0_gnn_ref(x, adj, W_w, W_b, a):
        import jax, jax.numpy as jnp
        import numpy as np
        B, IN_F, OUT_F, H = (1024, 256, 256, 8)
        D = OUT_F // H
        Bn = x.shape[0]
        h = (x @ W_w.T + W_b).reshape(Bn, H, D)
        a_src, a_dst = (a[:D, 0], a[D:, 0])
        s_src = jnp.einsum('bhd,d->bh', h, a_src)
        s_dst = jnp.einsum('bhd,d->bh', h, a_dst)
        e = jax.nn.leaky_relu(s_src[:, None, :] + s_dst[None, :, :], negative_slope=0.2)
        e = jnp.where(adj[:, :, None] == 0, jnp.float32(-1000000000.0), e)
        attn = jax.nn.softmax(e, axis=1)
        h_prime = jnp.einsum('ijh,jhd->ihd', attn, h).reshape(Bn, H * D)
        return jax.nn.elu(h_prime)

    def _L1_gnn_ref(x, adj, W_self, b_self, W_nb, b_nb, W_comb, b_comb):
        import jax, jax.numpy as jnp
        import numpy as np
        N, D_IN, D_OUT = (4096, 256, 256)
        mask = (adj > 0).astype(x.dtype)
        deg = jnp.sum(mask, axis=1, keepdims=True)
        agg = mask @ x / jnp.maximum(deg, 1.0)
        self_f = x @ W_self + b_self
        nb_f = agg @ W_nb + b_nb
        combined = jnp.concatenate([self_f, nb_f], axis=-1)
        out = combined @ W_comb + b_comb
        return jax.nn.relu(out)

    def _L2_gnn_ref(X, A, W_nb, b_nb, W_line, b_line, neibor_num):
        import jax, jax.numpy as jnp
        import numpy as np
        Ab = A > 0
        keep = Ab & (jnp.cumsum(Ab.astype(jnp.int32), axis=1) <= neibor_num)
        cnt = keep.sum(axis=1, keepdims=True).astype(X.dtype)
        nb_sum = keep.astype(X.dtype) @ X
        nb_mean = nb_sum / jnp.maximum(cnt, 1.0)
        xj = jax.nn.leaky_relu(nb_mean @ W_nb.T + b_nb)
        xi = jax.nn.leaky_relu(X @ W_line.T + b_line)
        return xi + jnp.where(cnt > 0, xj, jnp.zeros((), X.dtype))

    def _L3_gnn_ref(prop_state, A, in_W, in_b, out_W, out_b, r_W, r_b, z_W, z_b, h_W, h_b, o1_W, o1_b, o2_W, o2_b):
        import jax, jax.numpy as jnp
        import numpy as np
        N = 2048
        STATE_DIM = 256
        OUTPUT_DIM = 256
        N_STEPS = 5
        W_STD = 0.02

        def _lin_params(key, out_dim, in_dim):
            W = jax.random.normal(key, (out_dim, in_dim), dtype=jnp.float32) * W_STD
            b = jnp.zeros((out_dim,), dtype=jnp.float32)
            return (W, b)
        Af = A.astype(prop_state.dtype)
        AfT = Af.T
        state = prop_state
        for _ in range(N_STEPS):
            s_in = state @ in_W.T + in_b
            s_out = state @ out_W.T + out_b
            a_in = Af @ s_in
            a_out = AfT @ s_out
            a = jnp.concatenate([a_in, a_out, state], axis=-1)
            r = jax.nn.sigmoid(a @ r_W.T + r_b)
            z = jax.nn.sigmoid(a @ z_W.T + z_b)
            joined = jnp.concatenate([a_in, a_out, r * state], axis=-1)
            h_hat = jnp.tanh(joined @ h_W.T + h_b)
            state = (1.0 - z) * state + z * h_hat
        out = jnp.tanh(state @ o1_W.T + o1_b) @ o2_W.T + o2_b
        return out
    h = jnp.maximum(_layernorm(x, axis=-1), 0.0)
    x = x + _L0_gnn_ref(h, adj, L0_gnn_W_w, L0_gnn_W_b, L0_gnn_a)
    h = jnp.maximum(_layernorm(x, axis=-1), 0.0)
    x = x + _L1_gnn_ref(h, adj, L1_gnn_W_self, L1_gnn_b_self, L1_gnn_W_nb, L1_gnn_b_nb, L1_gnn_W_comb, L1_gnn_b_comb)
    h = jnp.maximum(_layernorm(x, axis=-1), 0.0)
    x = x + _L2_gnn_ref(h, adj, L2_gnn_W_nb, L2_gnn_b_nb, L2_gnn_W_line, L2_gnn_b_line, 64)
    h = jnp.maximum(_layernorm(x, axis=-1), 0.0)
    x = x + _L3_gnn_ref(h, adj, L3_gnn_in_W, L3_gnn_in_b, L3_gnn_out_W, L3_gnn_out_b, L3_gnn_r_W, L3_gnn_r_b, L3_gnn_z_W, L3_gnn_z_b, L3_gnn_h_W, L3_gnn_h_b, L3_gnn_o1_W, L3_gnn_o1_b, L3_gnn_o2_W, L3_gnn_o2_b)
    return x

_drawn_inputs = setup_inputs


def setup_inputs(seed=0):
    import zlib

    import numpy as np

    out = dict(_drawn_inputs(seed))
    spreads = {'L0_gnn_W_b': (0.0, 0.1),
     'L3_gnn_in_b': (0.0, 0.292),
     'L3_gnn_out_b': (0.0, 0.1),
     'L3_gnn_r_b': (0.0, 2.0),
     'L3_gnn_z_b': (0.0, 2.0),
     'L3_gnn_h_b': (0.0, 0.8),
     'L3_gnn_o1_b': (0.0, 0.332),
     'L3_gnn_o2_b': (0.0, 0.1)}
    factors = {'L1_gnn_b_self': 6.743,
     'L1_gnn_b_nb': 5.914,
     'L1_gnn_b_comb': 3.441,
     'L2_gnn_b_nb': 2.905,
     'L3_gnn_r_W': 64.0}
    for name, (base, spread) in spreads.items():
        noise = np.random.default_rng([zlib.crc32(name.encode()), seed]).standard_normal(out[name].shape)
        drawn = base * np.exp(spread * noise) if base else spread * noise
        out[name] = jnp.asarray(drawn.astype(out[name].dtype))
    for name, factor in factors.items():
        out[name] = (out[name] * factor).astype(out[name].dtype)
    return out
```

```python
import numpy as np
import concourse.bass as bass
from concourse import mybir
from contextlib import ExitStack



def gnn_stack_kernel(nc, x_in, adj_t, w, out):
    F32, F16, BF16, F8, U8 = (mybir.dt.float32, mybir.dt.float16, mybir.dt.bfloat16, mybir.dt.float8e4,
                              mybir.dt.uint8)
    ALU = mybir.AluOpType
    ACT = mybir.ActivationFunctionType
    AX = mybir.AxisListType
    RMAX = bass.bass_isa.ReduceOp.max

    P = 128
    N, D = x_in.shape
    T = N // P
    K = D // P
    H = 8
    DH = D // H
    E = DH + 1
    CH = 512
    NC = N // CH
    HALF = N // 2
    TH = T // 2
    CAP = 64.0
    STEPS = 5
    ST, WS, WQ = 16.0, 64.0, 1024.0
    PR = ST * WS
    UP = 8.0 * float(np.log(2.0))
    BIG = float(2.0 ** 60)
    EPS = 1e-5
    DC = D + 2 * H
    KB = K * D * 2 * 2

    ctx = ExitStack()
    with ctx:
        def sem(name):
            return ctx.enter_context(nc.semaphore(name))

        def sb(name, shape, dt):
            return ctx.enter_context(nc.sbuf_tensor(name, shape, dt))

        ARENA = 202752
        arena = sb("arena", [P, ARENA], U8)

        def at(off, n, dt):
            size = {F32: 4, F16: 2, BF16: 2, F8: 1}[dt]
            assert off % 4 == 0 and off + n * size <= ARENA
            return arena[:, off:off + n * size].bitcast(dt)

        AT_O = 0
        KD_O = AT_O + T * N * 2
        HN_O = KD_O + T * N
        HT_O = HN_O + 2 * T * D * 2
        Q_O = HT_O + 2 * T * D * 2
        DQ_O = Q_O + 2 * T * D * 2
        X_O = DQ_O + 2 * T * D * 2
        WA_O = X_O + T * D * 4

        AT = at(AT_O, T * N, BF16).rearrange("p (t n) -> p t n", t=T)
        KT = at(KD_O, T * N, F8).rearrange("p (t n) -> p t n", t=T)
        HN = at(HN_O, 2 * T * D, F16).rearrange("p (t s d) -> p t s d", t=T, s=2)
        HT = at(HT_O, 2 * T * D, F16).rearrange("p (s k n) -> p s k n", s=2, k=K)
        QT = at(Q_O, 2 * T * D, F16).rearrange("p (s k n) -> p s k n", s=2, k=K)
        X = at(X_O, T * D, F32).rearrange("p (t d) -> p t d", t=T)

        HT0 = at(HN_O, 2 * T * D, F16).rearrange("p (s k n) -> p s k n", s=2, k=K)
        HN0 = at(HT_O, 2 * T * D, F16).rearrange("p (t s d) -> p t s d", t=T, s=2)
        FTW = 4 * E
        FTF = at(HN_O, H * T * FTW, F16)
        FT = FTF.rearrange("p (h t e s c) -> p h t e s c", h=H, t=T, e=2, s=2)
        SBC_O = HN_O + H * T * FTW * 2
        SBC = at(SBC_O, 2 * HALF, F32).rearrange("p (b n) -> p b n", b=2)
        MS_O = SBC_O + 2 * HALF * 4
        NM = 8
        MS = at(MS_O, NM * HALF, BF16).rearrange("p (b n) -> p b n", b=NM)
        NY = 3
        YS_O = MS_O + NM * HALF * 2
        YS = at(YS_O, NY * HALF, BF16).rearrange("p (b n) -> p b n", b=NY)
        assert YS_O + NY * HALF * 2 <= X_O
        STG0 = at(MS_O, 2 * K * D, F32).rearrange("p (m k d) -> p m k d", m=2, k=K)
        SROW = at(SBC_O, N, F32)
        CS = at(DQ_O, 2 * N, F16).rearrange("p (b n) -> p b n", b=2)
        GR_O = DQ_O + 2 * N * 2
        GR = at(GR_O, 2 * H * 2 * E, F32).rearrange("p (b h e c) -> p b h e c", b=2, h=H, e=2)
        W0 = at(WA_O, 2 * K * DC, F16).rearrange("p (s k d) -> p s k d", s=2, k=K)
        HF_O = WA_O + 2 * K * DC * 2
        HF = at(HF_O, T * H * E, F32).rearrange("p (t h c) -> p t h c", t=T, h=H)
        TM_O = WA_O + 2 * K * DC * 2
        TSZ = TH * 3 * E
        TMP = at(TM_O, TSZ, F32).rearrange("p (t g c) -> p t g c", t=TH, g=3)
        TSUM = at(TM_O + TSZ * 4, TSZ, F32).rearrange("p (t g c) -> p t g c", t=TH, g=3)
        TA = at(TM_O + 2 * TSZ * 4, TH * E, F32).rearrange("p (t c) -> p t c", t=TH)
        TB = at(TM_O + 2 * TSZ * 4 + TH * E * 4, TH * E, F32).rearrange("p (t c) -> p t c", t=TH)
        TV_O = TM_O + 2 * TSZ * 4 + 2 * TH * E * 4
        TV, TN, TE, TP = (at(TV_O + n * TH * DH * 4, TH * DH, F32).rearrange("p (t c) -> p t c", t=TH)
                          for n in range(4))

        REC = at(TV_O + 4 * TH * DH * 4, TH, F32)

        def weight(n):
            return at(WA_O + n * KB, 2 * K * D, F16).rearrange("p (s k d) -> p s k d", s=2, k=K)

        W1S, W1Q, W2S, W2Q = (weight(n) for n in range(4))
        STG1 = at(DQ_O, 6 * K * D, F32).rearrange("p (m k d) -> p m k d", m=6, k=K)
        SF_O = DQ_O + 6 * K * D * 4
        SF = at(SF_O, 2 * D, F32).rearrange("p (b d) -> p b d", b=2)
        SV2 = at(SF_O + 2 * D * 4, 2 * D, F32).rearrange("p (b d) -> p b d", b=2)
        STG3 = at(KD_O, 13 * K * D, F32).rearrange("p (m k d) -> p m k d", m=13, k=K)
        WQG = [weight(n) for n in range(3)]
        WSG = [weight(n) for n in range(3, 6)]
        WO1, WO2 = weight(6), weight(7)
        ZR = at(X_O, 2 * K * CH, F32).rearrange("p (b k n) -> p b k n", b=2, k=K)
        RSB = at(X_O + 2 * K * CH * 4, 2 * 2 * K * CH, F16).rearrange("p (b s k n) -> p b s k n", b=2, s=2, k=K)
        RG = at(DQ_O, 2 * CH, F32).rearrange("p (b n) -> p b n", b=2)
        SG = at(KD_O + T * D * 4, 3 * K * CH, F32).rearrange("p (b k n) -> p b k n", b=3, k=K)
        HG = at(DQ_O + 8192, 2 * CH, F32).rearrange("p (b n) -> p b n", b=2)
        XF = at(KD_O, T * D, F32).rearrange("p (t d) -> p t d", t=T)
        OB = at(KD_O + T * D * 4, T * D, F32).rearrange("p (t d) -> p t d", t=T)

        ident = sb("ident", [P, P], F16)
        tri = sb("tri", [P, P], BF16)
        last_row = sb("last_row", [P, P], F16)
        ones = sb("ones", [P, P], F16)
        share = sb("share", [P, 2], F16)
        eps_c = sb("eps_c", [P, 1], F32)
        up_c = sb("up_c", [P, 1], F32)
        a_sel = sb("a_sel", [P, K, 2 * H], F32)
        b_col = sb("b_col", [P, 8 * K], F32)
        b_row = sb("b_row", [1, DC], F32)
        brow = sb("brow", [P, DC], F16)
        vcol = at(WA_O + 8 * KB, 3 * K, F32)
        bn_bc = at(WA_O + 4 * KB, D, F32)
        degb = sb("degb", [P, N], F16)
        stats = at(Q_O + 2 * D * 4, T * 6, F32).rearrange("p (t c) -> p t c", t=T)
        mv = sb("mv", [P, T, 2], F32)
        rstd = sb("rstd", [P, T], F32)
        nmr = sb("nmr", [P, T], F32)
        deg = sb("deg", [P, 6, T], F32)
        tb = sb("tb", [P, 4, H, T], F32)
        ts_ = at(GR_O + 2 * H * 2 * E * 4 + T * 2 * H * 4, 4 * H * T, F32).rearrange("p (n h t) -> p n h t", n=4, h=H)
        cm = sb("cm", [P, 2, H], F32)
        sv = at(GR_O + 2 * H * 2 * E * 4, T * 2 * H, F32).rearrange("p (t c) -> p t c", t=T)
        HSC = at(Q_O, 2 * D, F32).rearrange("p (b d) -> p b d", b=2)
        BIGS, NEGS, CA, CB = (tb[:, n] for n in range(4))
        E1, E2, SCR, SCM = (ts_[:, n] for n in range(4))

        PS = ctx.enter_context(nc.psum_tensor("ps", [P, 8, CH], F32))
        PS16 = [PS[:, b, :].bitcast(F16) for b in range(8)]

        bigs = sb("bigs", [P, 2, T], F32)
        bigs_in = sem("bigs_in")
        act_dummy = sb("act_dummy", [P, 2], F32)
        s_dram = nc.dram_tensor("source_scores", [H, N], F32, kind="Internal").ap()
        x_dram = nc.dram_tensor("residual", [N, D], F32, kind="Internal").ap()
        rows = "(t p) d -> p t d"

        consts = sem("consts")
        at_in = [sem(f"at_in{t}") for t in range(T // 2)]
        x_in_s = [sem(f"x_in{t}") for t in range(2)]
        w0_in, asel_in, asel_zero, b0_in = sem("w0_in"), sem("asel_in"), sem("asel_zero"), sem("b0_in")
        fold0, w0_hi, w0_lo = sem("fold0"), sem("w0_hi"), sem("w0_lo")
        brow_hi, brow_lo, brow_zero = sem("brow_hi"), sem("brow_lo"), sem("brow_zero")
        dve_c, act_c, pool_c = sem("dve_c"), sem("act_c"), sem("pool_c")
        per_layer = {"var": T, "std": 1, "norm": T + 3, "h_pre": T, "h_hi": T, "h_lo": T, "turned": T // 2,
                     "turn_a": T // 4, "turn_v": T // 4}
        ls = {k: sem(k) for k in per_layer}

        def wait_layer(eng, L, k, n):
            eng.wait_ge(ls[k], L * per_layer[k] + n)

        feat, feat_out, srow_mm, srow_out, srow_st = (sem("feat"), sem("feat_out"), sem("srow_mm"),
                                                      sem("srow_out"), sem("srow_st"))
        cmax_l, cmax, tabs_d, tabs_e, tabs = (sem("cmax_l"), sem("cmax"), sem("tabs_d"), sem("tabs_e"), sem("tabs"))
        g_done, ft_hi, ft_lo = sem("g_done"), sem("ft_hi"), sem("ft_lo")
        cum_mm, cum_cp, kept = sem("cum_mm"), sem("cum_cp"), sem("kept")
        degb_mm, degb_cp, deg_mm, deg_cp, deg_rd = (sem("degb_mm"), sem("degb_cp"), sem("deg_mm"),
                                                    sem("deg_cp"), sem("deg_rd"))
        sbc_in = [sem("sbc_in0"), sem("sbc_in1")]
        y_ready, m_ready, m_used = sem("y_ready"), sem("m_ready"), sem("m_used")
        lo_out, t_sum, t_used, share_out = sem("lo_out"), sem("t_sum"), sem("t_used"), sem("share_out")
        mix_a, mixed, divided, neg_ready, pos_ready, exp_ready, pos_added, x_heads = (sem(n) for n in (
            "mix_a", "mixed", "divided", "neg_ready", "pos_ready", "exp_ready", "pos_added", "x_heads"))
        w1_in, wc_mm, wc_hi, wc_lo = sem("w1_in"), sem("wc_mm"), sem("wc_hi"), sem("wc_lo")
        b1_mm, b1_hi, b1_lo, b1_in = sem("b1_mm"), sem("b1_hi"), sem("b1_lo"), sem("b1_in")
        q_mm = [sem(f"q_mm{n}") for n in range(3)]
        q_hi = [sem(f"q_hi{n}") for n in range(3)]
        q_lo = [sem(f"q_lo{n}") for n in range(3)]
        d_mm = [sem(f"d_mm{n}") for n in range(3)]
        d_sf = [sem(f"d_sf{n}") for n in range(3)]
        d_v = [sem(f"d_v{n}") for n in range(3)]
        d_x = [sem(f"d_x{n}") for n in range(3)]
        d_u = [sem(f"d_u{n}") for n in range(3)]
        b2_hi, b2_lo, d_xi, d_lr, up_a, up_b = sem("b2_hi"), sem("b2_lo"), sem("d_xi"), sem("d_lr"), sem("up_a"), sem("up_b")
        x_out, x_back = sem("x_out"), sem("x_back")
        w3_in, w3_mm, w3_hi, w3_lo = sem("w3_in"), sem("w3_mm"), sem("w3_hi"), sem("w3_lo")
        v_mm, v_hi = sem("v_mm"), sem("v_hi")
        rz_deg, h_deg = sem("rz_deg"), sem("h_deg")
        rz_mm, rz_act, st_r, rs_f, rs_hi, rs_lo, h_mm, h_act = (sem(n) for n in (
            "rz_mm", "rz_act", "st_r", "rs_f", "rs_hi", "rs_lo", "h_mm", "h_act"))
        new_f, new_hi, new_lo, back_mm, back_cp, state_c = (sem(n) for n in (
            "new_f", "new_hi", "new_lo", "back_mm", "back_cp", "state_c"))
        o1_mm, o1_act, o1_hi, o1_lo, o2_mm, o2_x, o2_out, bo_in, bo_hi, bo_lo = (sem(n) for n in (
            "o1_mm", "o1_act", "o1_hi", "o1_lo", "o2_mm", "o2_x", "o2_out", "bo_in", "bo_hi", "bo_lo"))

        PARTS = ((0, 0), (0, 1), (1, 0))
        block = ctx.enter_context(nc.Block())

        def mat(a):
            return a.rearrange("(k p) d -> p k d", p=P)

        ALONE = (2, 6, 10, 14)
        STARTED = [t for t in range(T) if t not in ALONE]
        NYH = len(STARTED)
        assert NYH % NY == 0 and T % NM == 0

        @block.sync
        def _(sp):
            x_v = x_in.rearrange(rows, p=P)
            for n in range(2):
                sp.dma_start(X[:, n * TH:(n + 1) * TH, :], x_v[:, n * TH:(n + 1) * TH, :]).then_inc(x_in_s[n], 16)
            sp.dma_start(STG0[:, 0], mat(w["l0_wt"])).then_inc(w0_in, 16)
            sp.dma_start(STG0[:, 1], mat(w["l0_w"])).then_inc(w0_in, 16)
            sp.dma_start(b_row[:, 0:D], w["l0_b"].rearrange("(a n) -> a n", a=1)).then_inc(b0_in, 16)
            sp.dma_start(b_col[:, 0:K], w["l0_b_c"]).then_inc(b0_in, 16)
            sp.wait_ge(asel_zero, 1)
            for h in range(H):
                for side in range(2):
                    sp.dma_start(a_sel[h % 4 * DH:(h % 4 + 1) * DH, h // 4, side * H + h:side * H + h + 1],
                                 w["l0_a"][side * DH:(side + 1) * DH, :]).then_inc(asel_in, 16)
            sp.wait_ge(srow_out, NC)
            sp.dma_start(s_dram[:, :], SROW[0:H, :]).then_inc(srow_st, 16)
            sp.wait_ge(srow_st, 16)

            def scores_of(h, b):
                sp.dma_start(SBC[:, b, :], s_dram[bass.ds(h, 1), b * HALF:(b + 1) * HALF]
                             .to_broadcast([P, HALF])).then_inc(sbc_in[b], 16)

            for b in range(2):
                scores_of(0, b)
            with sp.Fori(1, H) as h:
                for b in range(2):
                    sp.wait_ge(m_ready, h * (2 * T) + (b + 1) * T - 2 * T)
                    scores_of(h, b)
            sp.wait_ge(m_used, 2 * H * T)
            sp.wait_ge(x_heads, 2 * H)
            for n, name in enumerate(("l1_ws_t", "l1_wn_t", "l1_wc1", "l1_wc2", "l2_wl_t", "l2_wn_t")):
                sp.dma_start(STG1[:, n], mat(w[name])).then_inc(w1_in, 16)
            sp.dma_start(b_row[:, 0:D], w["l1_bc"].rearrange("(a n) -> a n", a=1)).then_inc(b1_in, 16)
            sp.dma_start(b_col[:, K:2 * K], w["l1_bs_c"]).then_inc(b1_in, 16)
            sp.dma_start(b_col[:, 2 * K:3 * K], w["l1_bn_c"]).then_inc(b1_in, 16)
            sp.dma_start(bn_bc[:, :], w["l2_bn"].rearrange("(a n) -> a n", a=1).to_broadcast([P, D]))\
                .then_inc(b1_in, 16)
            sp.wait_ge(b1_hi, 1)
            sp.wait_ge(b1_lo, 2)
            sp.dma_start(b_row[:, 0:D], w["l2_bl"].rearrange("(a n) -> a n", a=1)).then_inc(b1_in, 16)
            sp.wait_ge(d_x[2], T)
            sp.dma_start(x_dram.rearrange(rows, p=P), X).then_inc(x_out, 16)
            sp.wait_ge(q_mm[2], K * NC)
            names = ["l3_in_w", "l3_out_w"] + [f"l3_{g}_t{n}" for g in "rzh" for n in range(3)] \
                + ["l3_o1_t", "l3_o2_t"]
            for n, name in enumerate(names):
                sp.dma_start(STG3[:, n], mat(w[name])).then_inc(w3_in, 16)
            for n, name in enumerate(("l3_in_b", "l3_out_b", "l3_rb", "l3_zb", "l3_hb", "l3_o1b")):
                sp.dma_start(b_col[:, (n + 2) * K if n > 1 else n * K:(n + 3) * K if n > 1 else (n + 1) * K],
                             w[name + "_c"]).then_inc(w3_in, 16)
            sp.dma_start(b_row[:, 0:D], w["l3_o2b"].rearrange("(a n) -> a n", a=1)).then_inc(w3_in, 16)
            sp.wait_ge(w3_hi, 8)
            sp.wait_ge(w3_lo, 8)
            sp.wait_ge(v_mm, 3)
            sp.wait_ge(x_out, 16)
            sp.dma_start(XF, x_dram.rearrange(rows, p=P)).then_inc(x_back, 16)
            out_v = out.rearrange(rows, p=P)
            for t in range(T // 2):
                sp.wait_ge(o2_x, 2 * t + 2)
                sp.dma_start(out_v[:, 2 * t:2 * t + 2, :], OB[:, 2 * t:2 * t + 2, :]).then_inc(o2_out, 16)
            sp.wait_ge(o2_out, 16 * (T // 2))

        @block.gpsimd
        def _(pool):
            g = nc.gpsimd
            g.memset(a_sel[:, :, :], 0.0).then_inc(asel_zero, 1)
            g.memset(ones[:, :], 1.0).then_inc(pool_c, 1)
            g.memset(tri[:, :], 1.0).then_inc(pool_c, 1)
            g.memset(share[:, :], 1.0 / P).then_inc(pool_c, 1)
            g.memset(eps_c[:, :], EPS).then_inc(pool_c, 1)
            g.memset(up_c[:, :], UP).then_inc(pool_c, 1)
            g.memset(brow[:, :], 0.0).then_inc(brow_zero, 1)
            pool.wait_ge(pool_c, 5)
            g.affine_select(out=ident[:, :], in_=ones[:, :], compare_op=ALU.is_equal, fill=0.0, base=0,
                            pattern=[[-1, P]], channel_multiplier=1).then_inc(consts, 1)
            g.affine_select(out=tri[:, :], in_=tri[:, :], compare_op=ALU.is_ge, fill=0.0, base=0,
                            pattern=[[1, P]], channel_multiplier=-1).then_inc(consts, 1)
            g.affine_select(out=last_row[:, :], in_=ones[:, :], compare_op=ALU.is_ge, fill=0.0, base=1 - P,
                            pattern=[[0, P]], channel_multiplier=1).then_inc(consts, 1)
            pool.wait_ge(x_in_s[0], 16)
            pool.wait_ge(x_in_s[1], 16)
            pool.wait_ge(w0_in, 32)
            for t in range(T):
                g.dma_start(AT[:, t, :], adj_t[t * P:(t + 1) * P, :]).then_inc(at_in[t // 2], 16)
            g.memset(HF[:, :, :, DH:E], 1.0).then_inc(consts, 1)
            pool.wait_ge(cmax_l, 1)
            g.partition_all_reduce(cm[:, 1, :], cm[:, 0, :], P, RMAX).then_inc(cmax, 1)
            pool.wait_ge(tabs_e, 4)
            pool.wait_ge(feat_out, 2 * T)
            for t in range(T):
                if t >= 2:
                    pool.wait_ge(ft_lo, t - 1)
                for e, tab in ((0, E1), (1, E2)):
                    g.tensor_tensor(GR[:, t % 2, :, e, :], HF[:, t, :, :],
                                    tab[:, :, t:t + 1].to_broadcast([P, H, E]), ALU.mult).then_inc(g_done, 1)

            pool.wait_ge(ft_lo, T)

            def finish(h, half):
                lo = half * TH
                n = h * 2 + half + 1

                def per_source(tab, width):
                    return tab[:, bass.ds(h, 1), lo:lo + TH].rearrange("p a t -> p (a t)").unsqueeze(2)\
                        .to_broadcast([P, TH, width])

                pool.wait_ge(t_sum, n)
                g.tensor_tensor(TB, TSUM[:, :, 2, :], TSUM[:, :, 1, :], ALU.subtract).then_inc(mix_a, 1)
                g.tensor_tensor(TA, TSUM[:, :, 0, :], per_source(CA, E), ALU.mult).then_inc(mix_a, 1)
                pool.wait_ge(mix_a, 2 * n)
                g.tensor_tensor(TB, TB, per_source(CB, E), ALU.mult).then_inc(t_used, 1)
                pool.wait_ge(t_used, n)
                g.tensor_tensor(TA, TA, TB, ALU.add).then_inc(mixed, 1)
                pool.wait_ge(mixed, n)
                pool.wait_ge(share_out, n)
                g.tensor_tensor(TV, TA[:, :, 0:DH], REC[:, :].unsqueeze(2).to_broadcast([P, TH, DH]), ALU.mult)\
                    .then_inc(divided, 1)
                pool.wait_ge(divided, n)
                g.tensor_scalar(TN, TV, 0.0, None, ALU.min).then_inc(neg_ready, 1)
                g.tensor_scalar(TP, TV, 0.0, -1.0, ALU.max, ALU.add).then_inc(pos_ready, 1)
                pool.wait_ge(pos_ready, n)
                xs = X[:, lo:lo + TH, bass.ds(h * DH, DH)]
                g.tensor_tensor(xs, xs, TP, ALU.add).then_inc(pos_added, 1)
                pool.wait_ge(pos_added, n)
                pool.wait_ge(exp_ready, n)
                g.tensor_tensor(xs, xs, TE, ALU.add).then_inc(x_heads, 1)

            for h in range(H):
                for half in range(2):
                    finish(h, half)
            for t in range(T):
                pool.wait_ge(d_xi, t + 1)
                g.tensor_tensor(X[:, t, :], X[:, t, :], SF[:, t % 2, :], ALU.add).then_inc(d_u[2], 1)

        def norm_vector(L, hn, x_wait):
            v = nc.vector
            for t in range(T):
                x_wait(nc.vector, t)
                v.bn_stats(stats[:, t, :], X[:, t, :]).then_inc(ls["var"], 1)
            for t in range(T):
                wait_layer(nc.vector, L, "var", t + 1)
                v.bn_aggr(mv[:, t, :], stats[:, t, :]).then_inc(ls["norm"], 1)
            wait_layer(nc.vector, L, "norm", T)
            wait_layer(nc.vector, L, "std", 1)
            v.reciprocal(rstd[:, :], nmr[:, :]).then_inc(ls["norm"], 1)
            wait_layer(nc.vector, L, "norm", T + 1)
            v.tensor_scalar(rstd[:, :], rstd[:, :], ST, None, ALU.mult).then_inc(ls["norm"], 1)
            wait_layer(nc.vector, L, "norm", T + 2)
            v.scalar_tensor_tensor(nmr[:, :], mv[:, :, 0], -1.0, rstd[:, :], ALU.mult, ALU.mult)\
                .then_inc(ls["norm"], 1)
            wait_layer(nc.vector, L, "norm", T + 3)
            for t in range(T):
                if t >= 2:
                    wait_layer(nc.vector, L, "h_lo", t - 1)
                v.tensor_scalar(HSC[:, t % 2, :], X[:, t, :], rstd[:, t:t + 1], nmr[:, t:t + 1],
                                ALU.mult, ALU.add).then_inc(ls["h_pre"], 1)
                if t >= 1:
                    norm_low(L, hn, t - 1)
            norm_low(L, hn, T - 1)

        def norm_low(L, hn, t):
            wait_layer(nc.vector, L, "h_pre", t + 1)
            wait_layer(nc.vector, L, "h_hi", t + 1)
            nc.vector.scalar_tensor_tensor(hn[:, t, 1, :], HSC[:, t % 2, :], 0.0, hn[:, t, 0, :],
                                           ALU.max, ALU.subtract).then_inc(ls["h_lo"], 1)

        def norm_scalar(L, hn):
            wait_layer(nc.scalar, L, "norm", T)
            nc.scalar.activation(nmr[:, :], mv[:, :, 1], ACT.Sqrt, bias=eps_c[:, :]).then_inc(ls["std"], 1)
            wait_layer(nc.scalar, L, "norm", T + 3)
            for t in range(T):
                nc.scalar.activation(hn[:, t, 0, :], X[:, t, :], ACT.Relu, bias=nmr[:, t:t + 1],
                                     scale=rstd[:, t:t + 1]).then_inc(ls["h_hi"], 1)

        def turn_tensor(L, hn):
            for q in range(T // 2):
                if q >= 2:
                    wait_layer(nc.tensor, L, "turn_a" if q % 2 else "turn_v", q // 2)
                for i in range(2):
                    t = 2 * q + i
                    wait_layer(nc.tensor, L, "h_hi", t + 1)
                    wait_layer(nc.tensor, L, "h_lo", t + 1)
                    for s in range(2):
                        for k in range(K):
                            mm = nc.tensor.transpose(
                                PS16[4 + q % 2][:, (s * K + k) * 256 + i * P:(s * K + k) * 256 + (i + 1) * P],
                                hn[:, t, s, k * P:(k + 1) * P], ident[:, :])
                mm.then_inc(ls["turned"], 1)

        def turn_copy(L, ht, q):
            dst = ht.rearrange("p s k n -> p (s k) n")[:, :, q * 256:(q + 1) * 256]
            src = PS16[4 + q % 2].rearrange("p (s n) -> p s n", s=4)
            if q % 2:
                wait_layer(nc.scalar, L, "turned", q + 1)
                nc.scalar.activation(dst, src, ACT.Copy).then_inc(ls["turn_a"], 1)
            else:
                wait_layer(nc.vector, L, "turned", q + 1)
                nc.vector.tensor_copy(dst, src).then_inc(ls["turn_v"], 1)

        def turned(eng, L):
            wait_layer(eng, L, "turn_a", T // 4)
            wait_layer(eng, L, "turn_v", T // 4)

        def sum_tensor(adj, hn, mm_sem, count0, free=None):
            for n in range(K * NC):
                c, k = n // K, n % K
                if free:
                    free(n)
                for t in range(T):
                    for s in range(2):
                        mm = nc.tensor.matmul(PS[:, n, :], hn[:, t, s, k * P:(k + 1) * P],
                                              adj[:, t, c * CH:(c + 1) * CH], start=(t == 0 and s == 0),
                                              stop=(t == T - 1 and s == 1))
                mm.then_inc(mm_sem, 1)

        def sum_scalar(n, mm_sem, hi_sem, base):
            c, k = n // K, n % K
            nc.scalar.wait_ge(mm_sem, base + n + 1)
            nc.scalar.activation(QT[:, 0, k, c * CH:(c + 1) * CH], PS[:, n, :], ACT.Copy, scale=1.0 / ST)\
                .then_inc(hi_sem, 1)

        def sum_vector(n, mm_sem, hi_sem, lo_sem, base):
            c, k = n // K, n % K
            nc.vector.wait_ge(hi_sem, base + n + 1)
            nc.vector.scalar_tensor_tensor(QT[:, 1, k, c * CH:(c + 1) * CH], PS[:, n, :], 1.0 / ST,
                                           QT[:, 0, k, c * CH:(c + 1) * CH], ALU.mult, ALU.subtract)\
                .then_inc(lo_sem, 1)

        def rows_tensor(dst, src, wt, t, width, bias):
            for k in range(K):
                for a, b in PARTS:
                    mm = nc.tensor.matmul(dst, src[:, a, k, t * P:(t + 1) * P], wt[:, b, k, 0:width],
                                          start=(k == 0 and a == b == 0),
                                          stop=(not bias and k == K - 1 and a == 1))
            if bias:
                mm = nc.tensor.matmul(dst, ones[:, :], brow[:, 0:width], start=False, stop=True)
            return mm

        @block.tensor
        def _(pe):
            t_ = nc.tensor
            pe.wait_ge(w0_in, 32)
            pe.wait_ge(asel_in, 16 * 2 * H)
            pe.wait_ge(b0_in, 32)
            for dk in range(K):
                for k in range(K):
                    t_.matmul(PS[:, 7, dk * 2 * H:(dk + 1) * 2 * H], STG0[:, 1, k, dk * P:(dk + 1) * P],
                              a_sel[:, k, :], start=(k == 0), stop=(k == K - 1))
            for k in range(K):
                mm = t_.matmul(PS[0:1, 7, 4 * H:6 * H], b_col[:, k:k + 1], a_sel[:, k, :],
                               start=(k == 0), stop=(k == K - 1))
            mm.then_inc(fold0, 1)
            pe.wait_ge(consts, 4)
            turn_tensor(0, HN0)
            turned(pe, 0)
            pe.wait_ge(w0_hi, 2)
            pe.wait_ge(w0_lo, 2)
            pe.wait_ge(brow_hi, 2)
            pe.wait_ge(brow_lo, 2)
            for t in range(T):
                if t >= 2:
                    pe.wait_ge(feat_out, 2 * (t - 1))
                rows_tensor(PS[:, 6 + t % 2, 0:DC], HT0, W0, t, DC, True).then_inc(feat, 1)
            for c in range(NC):
                if c == 0:
                    pe.wait_ge(feat_out, 2 * T)
                if c >= 2:
                    pe.wait_ge(srow_out, c - 1)
                for k in range(K):
                    for a, b in PARTS:
                        t_.matmul(PS[0:H, 6 + c % 2, :], W0[:, a, k, D:D + H], HT0[:, b, k, c * CH:(c + 1) * CH],
                                  start=(k == 0 and a == b == 0), stop=False)
                t_.matmul(PS[0:H, 6 + c % 2, :], brow[:, D:D + H],
                          ones[:, :].unsqueeze(1).to_broadcast([P, CH // P, P]),
                          start=False, stop=True).then_inc(srow_mm, 1)
            for t in range(T):
                pe.wait_ge(at_in[t // 2], 32)
                for c in range(NC):
                    if t >= 1:
                        pe.wait_ge(cum_cp, 2 * (t - 1) + c // 2 + 1)
                    mm = t_.matmul(PS[:, c, :], tri[:, :], AT[:, t, c * CH:(c + 1) * CH], start=True, stop=(t == 0))
                    if t >= 1:
                        mm = t_.matmul(PS[:, c, :], last_row[:, :], CS[:, (t - 1) % 2, c * CH:(c + 1) * CH],
                                       start=False, stop=True)
                    mm.then_inc(cum_mm, 1)
            for c in range(NC):
                pe.wait_ge(cum_cp, 2 * T)
                t_.matmul(PS[:, c, :], last_row[:, :], CS[:, (T - 1) % 2, c * CH:(c + 1) * CH],
                          start=True, stop=True).then_inc(degb_mm, 1)
            pe.wait_ge(degb_cp, NC)
            for t in range(T):
                mm = t_.matmul(PS[:, 4, t:t + 1], degb[:, t * P:(t + 1) * P], share[:, 0:1], start=True, stop=True)
            mm.then_inc(deg_mm, 1)
            pe.wait_ge(deg_cp, 1)
            pe.wait_ge(ft_hi, T)
            pe.wait_ge(ft_lo, T)


            def head_tensor(h, first):
                for half in range(2):
                    if not first:
                        pe.wait_ge(t_sum, h * 2 + half - 1)
                    for t in range(T):
                        ft = h * (T * FTW) + t * FTW
                        for i in range(TH):
                            t_.matmul(PS[:, 4 * half + i // 2, i % 2 * 256 + 4 * E:i % 2 * 256 + 6 * E],
                                      AT[:, t, half * HALF + i * P:half * HALF + (i + 1) * P],
                                      FTF[:, bass.ds(ft + 2 * E, 2 * E)],
                                      start=(t == 0 and i % 2 == 0), stop=False, skip_group_check=True)
                        pe.wait_ge(m_ready, h * (2 * T) + half * T + t + 1)
                        for i in range(TH):
                            mm = t_.matmul(PS[:, 4 * half + i // 2, i % 2 * 256:i % 2 * 256 + 4 * E],
                                           MS[:, t % NM, i * P:(i + 1) * P], FTF[:, bass.ds(ft, FTW)],
                                           start=False, stop=(t == T - 1), skip_group_check=True)
                        mm.then_inc(m_used, 1)

            head_tensor(0, True)
            with pe.Fori(1, H) as h:
                head_tensor(h, False)

            pe.wait_ge(w1_in, 16 * 6)
            pe.wait_ge(b1_in, 16 * 4)
            pe.wait_ge(t_sum, 2 * H)
            for m in range(2):
                for dk in range(K):
                    for k in range(K):
                        mm = t_.matmul(PS[:, m, dk * D:(dk + 1) * D], STG1[:, m, k, dk * P:(dk + 1) * P],
                                       STG1[:, 2 + m, k, :], start=(k == 0), stop=(k == K - 1))
                mm.then_inc(wc_mm, 1)
            for m in range(2):
                for k in range(K):
                    mm = t_.matmul(PS[0:1, 2, 0:D], b_col[:, (m + 1) * K + k:(m + 1) * K + k + 1],
                                   STG1[:, 2 + m, k, :], start=(m == k == 0), stop=(m == 1 and k == K - 1))
            mm.then_inc(b1_mm, 1)
            for L in (1, 2):
                turn_tensor(L, HN)
                turned(pe, L)
                if L == 1:
                    pe.wait_ge(wc_hi, 4)
                    pe.wait_ge(wc_lo, 4)
                    pe.wait_ge(b1_hi, 1)
                    pe.wait_ge(b1_lo, 2)
                else:
                    pe.wait_ge(b2_hi, 1)
                    pe.wait_ge(b2_lo, 1)
                sum_tensor(AT if L == 1 else KT, HN, q_mm[L], 0)
                for t in range(T):
                    pe.wait_ge(q_lo[L], K * NC if t else K * NC)
                    if t >= 2:
                        pe.wait_ge(d_v[L], t - 1)
                        pe.wait_ge(d_sf[L], t - 1)
                    rows_tensor(PS[:, t % 2, 0:D], HT, W1S if L == 1 else W2S, t, D, True)
                    rows_tensor(PS[:, t % 2, D:2 * D], QT, W1Q if L == 1 else W2Q, t, D, False)\
                        .then_inc(d_mm[L], 1)

            pe.wait_ge(w3_in, 16 * 20)
            pe.wait_ge(d_v[2], T)
            pe.wait_ge(d_sf[2], T)
            for g in range(3):
                for dk in range(K):
                    n = 0
                    for m in range(2):
                        for k in range(K):
                            mm = t_.matmul(PS[:, g, dk * D:(dk + 1) * D], STG3[:, m, k, dk * P:(dk + 1) * P],
                                           STG3[:, 2 + 3 * g + m, k, :], start=(n == 0), stop=(n == 3))
                            n += 1
                mm.then_inc(w3_mm, 1)
            for g in range(3):
                for k2 in range(K):
                    n = 0
                    for m in range(2):
                        for k in range(K):
                            mm = t_.matmul(PS[:, 6, g * K + k2:g * K + k2 + 1],
                                           STG3[:, 2 + 3 * g + m, k, k2 * P:(k2 + 1) * P],
                                           b_col[:, m * K + k:m * K + k + 1], start=(n == 0), stop=(n == 3))
                            n += 1
                mm.then_inc(v_mm, 1)
            turn_tensor(3, HN)
            turned(pe, 3)
            pe.wait_ge(w3_hi, 8)
            pe.wait_ge(w3_lo, 8)
            pe.wait_ge(v_hi, 1)

            def gate_tensor(bank, gate, k2, c, state, cols):
                o = slice(k2 * P, (k2 + 1) * P)
                for k in range(K):
                    for a, b in PARTS:
                        t_.matmul(PS[:, bank, :], WQG[gate][:, a, k, o], QT[:, b, k, c * CH:(c + 1) * CH],
                                  start=(k == 0 and a == b == 0), stop=False)
                for k in range(K):
                    for a, b in PARTS:
                        mm = t_.matmul(PS[:, bank, :], WSG[gate][:, a, k, o], state[:, b, k, cols],
                                       start=False, stop=(k == K - 1 and a == 1))
                return mm

            def step_sums(step, after):
                def part(n, t0, t1):
                    c, k = n // K, n % K
                    for t in range(t0, t1):
                        for s in range(2):
                            mm = t_.matmul(PS[:, n, :], HN[:, t, s, k * P:(k + 1) * P],
                                           AT[:, t, c * CH:(c + 1) * CH], start=(t == 0 and s == 0),
                                           stop=(t == T - 1 and s == 1))
                    if t1 == T:
                        mm.then_inc(q_mm[0], 1)

                if after:
                    for n in range(3):
                        pe.wait_ge(rz_act, step * (4 * NC) - K * 2 + n + 1)
                        pe.wait_ge(back_cp, step * (2 * NC) - 4)
                        part(n, 0, T // 2)
                    back(step - 1, NC - 2)
                    pe.wait_ge(rz_act, step * (4 * NC))
                    part(3, 0, T // 2)
                    for n in range(4):
                        pe.wait_ge(back_cp, step * (2 * NC) - 2)
                        part(n, T // 2, T - 4)
                    back(step - 1, NC - 1)
                    for n in range(4):
                        pe.wait_ge(back_cp, step * (2 * NC))
                        part(n, T - 4, T)
                for n in range(4 if after else 0, K * NC):
                    part(n, 0, T)

            def back(step, c):
                for q in range(2):
                    if c == 0:
                        pe.wait_ge(q_lo[0], step * (K * NC) + 6 + q + 1)
                    else:
                        pe.wait_ge(back_cp, step * (2 * NC) + 2 * (c - 1) + q + 1)
                    pe.wait_ge(new_hi, step * (K * NC) + K * (c + 1))
                    pe.wait_ge(new_lo, step * (K * NC) + K * (c + 1))
                    for i in range(2):
                        t = 4 * c + 2 * q + i
                        for s in range(2):
                            for k in range(K):
                                mm = t_.transpose(
                                    PS16[6 + q][:, i * 2 * D + s * D + k * P:i * 2 * D + s * D + (k + 1) * P],
                                    HT[:, s, k, t * P:(t + 1) * P], ident[:, :])
                    mm.then_inc(back_mm, 1)

            def step_gates(step, last):
                def rz(c):
                    pe.wait_ge(q_lo[0], (step + 1) * (K * NC) if c == NC - 1 else step * (K * NC) + K * (c + 1))
                    for gate in range(2):
                        for k2 in range(K):
                            bank = gate * K + k2
                            if c == 0:
                                pe.wait_ge(q_lo[0], step * (K * NC) + bank + 1)
                            else:
                                pe.wait_ge(rz_act, step * (4 * NC) + 4 * (c - 1) + bank + 1)
                            gate_tensor(bank, gate, k2, c, HT, slice(c * CH, (c + 1) * CH)).then_inc(rz_mm, 1)

                def hg(c):
                    pe.wait_ge(rs_hi, step * (K * NC) + K * (c + 1))
                    pe.wait_ge(rs_lo, step * (K * NC) + K * (c + 1))
                    for k2 in range(K):
                        if c == 0:
                            pe.wait_ge(q_lo[0], step * (K * NC) + 4 + k2 + 1)
                        else:
                            pe.wait_ge(h_act, step * (K * NC) + K * (c - 1) + k2 + 1)
                        gate_tensor(4 + k2, 2, k2, c, RSB[:, c % 2], slice(0, CH)).then_inc(h_mm, 1)

                rz(0)
                rz(1)
                hg(0)
                rz(2)
                hg(1)
                if not last:
                    back(step, 0)
                rz(3)
                hg(2)
                if not last:
                    back(step, 1)
                hg(3)

            pe.wait_ge(state_c, 1)
            step_sums(0, False)
            with pe.Fori(0, STEPS - 1) as step:
                step_gates(step, False)
                step_sums(step + 1, True)
            step_gates(STEPS - 1, True)

            pe.wait_ge(rz_act, STEPS * 4 * NC)
            pe.wait_ge(h_act, STEPS * K * NC)
            for n in range(K * NC):
                c, k2 = n // K, n % K
                pe.wait_ge(new_hi, ((STEPS - 1) * NC + c + 1) * K)
                pe.wait_ge(new_lo, ((STEPS - 1) * NC + c + 1) * K)
                o = slice(k2 * P, (k2 + 1) * P)
                for k in range(K):
                    for a, b in PARTS:
                        mm = t_.matmul(PS[:, n, :], WO1[:, a, k, o], HT[:, b, k, c * CH:(c + 1) * CH],
                                       start=(k == 0 and a == b == 0), stop=(k == K - 1 and a == 1))
                mm.then_inc(o1_mm, 1)
            pe.wait_ge(bo_hi, 1)
            pe.wait_ge(bo_lo, 1)
            for t in range(T):
                pe.wait_ge(o1_lo, K * NC)
                if t >= 2:
                    pe.wait_ge(o2_x, t - 1)
                rows_tensor(PS[:, t % 2, 0:D], QT, WO2, t, D, True).then_inc(o2_mm, 1)

        @block.scalar
        def _(act):
            a_ = nc.scalar
            pool_wait = act.wait_ge
            pool_wait(pool_c, 5)
            pool_wait(brow_zero, 1)
            act.wait_ge(w0_in, 32)
            act.wait_ge(b0_in, 32)
            a_.activation(W0[:, 0, :, 0:D], STG0[:, 0], ACT.Copy, scale=WS).then_inc(w0_hi, 1)
            a_.activation(brow[0:1, 0:D], b_row[:, 0:D], ACT.Copy, scale=PR).then_inc(brow_hi, 1)
            act.wait_ge(fold0, 1)
            a_.activation(W0[:, 0, :, D:DC], PS[:, 7, 0:4 * H].rearrange("p (k c) -> p k c", k=K), ACT.Copy,
                          scale=WS).then_inc(w0_hi, 1)
            a_.activation(brow[0:1, D:DC], PS[0:1, 7, 4 * H:6 * H], ACT.Copy, scale=PR).then_inc(brow_hi, 1)
            norm_scalar(0, HN0)
            for q in range(1, T // 2, 2):
                turn_copy(0, HT0, q)
            for t in range(T):
                act.wait_ge(feat, t + 1)
                if t == 0:
                    act.wait_ge(consts, 4)
                a_.activation(HF[:, t, :, 0:DH], PS[:, 6 + t % 2, 0:D].rearrange("p (h c) -> p h c", h=H),
                              ACT.Copy, scale=1.0 / PR).then_inc(feat_out, 1)
                a_.activation(sv[:, t, :], PS[:, 6 + t % 2, D:DC], ACT.Copy, scale=1.0 / PR).then_inc(feat_out, 1)
            for c in range(NC):
                act.wait_ge(srow_mm, c + 1)
                a_.activation(SROW[0:H, c * CH:(c + 1) * CH], PS[0:H, 6 + c % 2, :], ACT.Copy, scale=1.0 / PR)\
                    .then_inc(srow_out, 1)
            act.wait_ge(tabs_d, 1)
            a_.activation(E1, SCR, ACT.Exp, bias=up_c[:, :]).then_inc(tabs_e, 1)
            a_.activation(E2, SCR, ACT.Exp, bias=up_c[:, :], scale=0.2).then_inc(tabs_e, 1)
            act.wait_ge(tabs, 5)
            a_.activation(CA, CA, ACT.Exp).then_inc(tabs_e, 1)
            a_.activation(CB, CB, ACT.Exp).then_inc(tabs_e, 1)
            for t in range(T):
                act.wait_ge(g_done, 2 * t + 2)
                a_.activation(FT[:, :, t, :, 0, :], GR[:, t % 2], ACT.Copy).then_inc(ft_hi, 1)
            for t in range(T):
                for c in range(2):
                    act.wait_ge(cum_mm, NC * t + 2 * c + 2)
                    if t >= 2:
                        act.wait_ge(kept, t - 1)
                    a_.activation(CS[:, t % 2, c * HALF:(c + 1) * HALF].rearrange("p (b n) -> p b n", b=2),
                                  PS[:, 2 * c:2 * c + 2, :], ACT.Copy).then_inc(cum_cp, 1)
            for c in range(NC):
                act.wait_ge(degb_mm, c + 1)
                a_.activation(degb[:, c * CH:(c + 1) * CH], PS[:, c, :], ACT.Copy).then_inc(degb_cp, 1)
            act.wait_ge(kept, T)
            act.wait_ge(deg_cp, 1)

            def low_out(h, half):
                act.wait_ge(m_used, h * (2 * T) + (half + 1) * T)
                if not (isinstance(h, int) and h == 0 and half == 0):
                    act.wait_ge(t_sum, h * 2 + half)
                a_.activation(TMP, PS[:, 4 * half:4 * half + 4, :].rearrange("p b (i n) -> p (b i) n", i=2)
                              [:, :, 0:6 * E].rearrange("p t (g s c) -> p t g s c", g=3, s=2)[:, :, :, 1, :],
                              ACT.Copy).then_inc(lo_out, 1)

            def elu_exp(h, half):
                act.wait_ge(neg_ready, h * 2 + half + 1)
                if not (isinstance(h, int) and h == 0 and half == 0):
                    act.wait_ge(x_heads, h * 2 + half)
                a_.activation(TE, TN, ACT.Exp).then_inc(exp_ready, 1)

            def head_scalar(h, first):
                for half in range(2):
                    a_.activation(bigs[:, half, :], BIGS[:, bass.ds(h, 1), :].rearrange("p a t -> p (a t)"),
                                  ACT.Copy).then_inc(bigs_in, 1)
                    act.wait_ge(bigs_in, h * 2 + half + 1)
                    act.wait_ge(sbc_in[half], h * 16 + 16)
                    n = 0
                    for t in range(T):
                        if t in ALONE:
                            continue
                        if n == 2 and not (first and half == 0):
                            low_out(h - (half == 0), 1 - half)
                        if n == 9 and not (first and half == 0):
                            elu_exp(h - (half == 0), 1 - half)
                        f = half * NYH + n - NY
                        if f >= 0:
                            act.wait_ge(m_ready, h * (2 * T) + f // NYH * T + STARTED[f % NYH] + 1)
                        elif not first:
                            act.wait_ge(m_ready, h * (2 * T) + STARTED[NYH + f] + 1 - T)
                        a_.activation(YS[:, n % NY, :], SBC[:, half, :], ACT.Relu, scale=BIG,
                                      bias=bigs[:, half, t:t + 1])\
                            .then_inc(y_ready, 1)
                        n += 1

            head_scalar(0, True)
            with act.Fori(1, H) as h:
                head_scalar(h, False)
            low_out(H - 1, 1)
            elu_exp(H - 1, 1)
            act.wait_ge(wc_mm, 2)
            for m, wt in ((0, W1S), (1, W1Q)):
                a_.activation(wt[:, 0], PS[:, m, :].rearrange("p (k d) -> p k d", k=K), ACT.Copy,
                              scale=(WS, WQ)[m]).then_inc(wc_hi, 1)
            for m, wt in ((0, W2S), (1, W2Q)):
                a_.activation(wt[:, 0], STG1[:, 4 + m], ACT.Copy, scale=(WS, WQ)[m]).then_inc(wc_hi, 1)
            act.wait_ge(b1_lo, 1)
            a_.activation(brow[0:1, 0:D], b_row[:, 0:D], ACT.Copy, scale=PR).then_inc(b1_hi, 1)
            for L in (1, 2):
                norm_scalar(L, HN)
                for q in range(1, T // 2, 2):
                    turn_copy(L, HT, q)
                for n in range(K * NC):
                    sum_scalar(n, q_mm[L], q_hi[L], 0)
                if L == 1:
                    for t in range(T):
                        act.wait_ge(d_mm[1], t + 1)
                        if t >= 2:
                            act.wait_ge(d_v[1], t - 1)
                        a_.activation(SF[:, t % 2, :], PS[:, t % 2, 0:D], ACT.Copy, scale=1.0 / PR)\
                            .then_inc(d_sf[1], 1)
                    act.wait_ge(b1_in, 16 * 5)
                    act.wait_ge(d_mm[1], T)
                    a_.activation(brow[0:1, 0:D], b_row[:, 0:D], ACT.Copy, scale=PR).then_inc(b2_hi, 1)
                else:
                    for t in range(T):
                        act.wait_ge(d_mm[2], t + 1)
                        if t >= 2:
                            act.wait_ge(d_u[2], t - 1)
                        a_.activation(SF[:, t % 2, :], PS[:, t % 2, 0:D], ACT.Copy, scale=1.0 / PR)\
                            .then_inc(d_sf[2], 1)
            act.wait_ge(w3_mm, 3)
            for g in range(3):
                a_.activation(WQG[g][:, 0], PS[:, g, :].rearrange("p (k d) -> p k d", k=K), ACT.Copy, scale=WQ)\
                    .then_inc(w3_hi, 1)
            for g in range(3):
                a_.activation(WSG[g][:, 0], STG3[:, 4 + 3 * g], ACT.Copy, scale=WS).then_inc(w3_hi, 1)
            for m, wt in ((11, WO1), (12, WO2)):
                a_.activation(wt[:, 0], STG3[:, m], ACT.Copy, scale=WS).then_inc(w3_hi, 1)
            act.wait_ge(v_mm, 3)
            a_.activation(vcol[:, :], PS[:, 6, 0:3 * K], ACT.Copy, scale=PR).then_inc(v_hi, 1)
            a_.activation(brow[0:1, 0:D], b_row[:, 0:D], ACT.Copy, scale=PR).then_inc(bo_hi, 1)
            norm_scalar(3, HN)
            for q in range(1, T // 2, 2):
                turn_copy(3, HT, q)
            act.wait_ge(x_out, 16)
            act.wait_ge(x_back, 16)
            wait_layer(act, 3, "h_lo", T)
            turned(act, 3)
            a_.activation(act_dummy[:, 0:1], eps_c[:, :], ACT.Copy).then_inc(state_c, 1)

            def gates_scalar(step, last):
                def gates(c):
                    for gate in range(2):
                        for k2 in range(K):
                            n = 4 * c + gate * K + k2
                            act.wait_ge(rz_deg, step * (4 * NC) + n + 1)
                            if gate == 0:
                                dst = RG[:, k2, :]
                                if c >= 1:
                                    act.wait_ge(rs_lo, step * (K * NC) + K * (c - 1) + k2 + 1)
                            else:
                                dst = ZR[:, c % 2, k2, :]
                                if c >= 2:
                                    act.wait_ge(new_f, step * (K * NC) + K * (c - 2) + k2 + 1)
                            a_.activation(dst, PS[:, gate * K + k2, :], ACT.Sigmoid, scale=1.0 / PR,
                                          bias=b_col[:, (4 + gate) * K + k2:(4 + gate) * K + k2 + 1])\
                                .then_inc(rz_act, 1)

                def rs_high(c):
                    for k2 in range(K):
                        act.wait_ge(rs_f, step * (K * NC) + K * c + k2 + 1)
                        a_.activation(RSB[:, c % 2, 0, k2, :], RG[:, k2, :], ACT.Copy).then_inc(rs_hi, 1)

                def tanh(c):
                    for k2 in range(K):
                        n = K * c + k2
                        act.wait_ge(h_deg, step * (K * NC) + n + 1)
                        if c >= 1:
                            act.wait_ge(new_lo, step * (K * NC) + n - 1)
                        a_.activation(HG[:, k2, :], PS[:, 4 + k2, :], ACT.Tanh, scale=1.0 / PR,
                                      bias=b_col[:, 6 * K + k2:6 * K + k2 + 1]).then_inc(h_act, 1)

                def new_high(c):
                    for k2 in range(K):
                        n = K * c + k2
                        act.wait_ge(new_f, step * (K * NC) + n + 1)
                        a_.activation(HT[:, 0, k2, c * CH:(c + 1) * CH], HG[:, k2, :], ACT.Copy)\
                            .then_inc(new_hi, 1)

                def back_out(c):
                    for q in range(2):
                        act.wait_ge(back_mm, step * (2 * NC) + 2 * c + q + 1)
                        t = 4 * c + 2 * q
                        a_.activation(HN[:, t:t + 2].rearrange("p t s d -> p (t s d)"), PS16[6 + q], ACT.Copy)\
                            .then_inc(back_cp, 1)

                gates(0)
                rs_high(0)
                gates(1)
                rs_high(1)
                tanh(0)
                new_high(0)
                gates(2)
                rs_high(2)
                tanh(1)
                new_high(1)
                if not last:
                    back_out(0)
                gates(3)
                rs_high(3)
                tanh(2)
                new_high(2)
                if not last:
                    back_out(1)
                tanh(3)
                if not last:
                    back_out(2)
                new_high(3)
                if not last:
                    back_out(3)

            def sums_scalar(step):
                for n in range(K * NC):
                    sum_scalar(n, q_mm[0], q_hi[0], step * (K * NC))

            sums_scalar(0)
            with act.Fori(0, STEPS - 1) as step:
                gates_scalar(step, False)
                sums_scalar(step + 1)
            gates_scalar(STEPS - 1, True)

            act.wait_ge(new_lo, STEPS * K * NC)
            for n in range(K * NC):
                c, k2 = n // K, n % K
                act.wait_ge(o1_mm, n + 1)
                if n >= 2:
                    act.wait_ge(o1_lo, n - 1)
                a_.activation(HG[:, n % 2, :], PS[:, n, :], ACT.Tanh, scale=1.0 / PR,
                              bias=b_col[:, 7 * K + k2:7 * K + k2 + 1]).then_inc(o1_act, 1)
                act.wait_ge(o1_act, n + 1)
                a_.activation(QT[:, 0, k2, c * CH:(c + 1) * CH], HG[:, n % 2, :], ACT.Copy, scale=ST)\
                    .then_inc(o1_hi, 1)


        @block.vector
        def _(dve):
            v = nc.vector

            def sync(sem_, n):
                dve.wait_ge(sem_, n)

            def split_low(lo, src, scale, hi):
                return v.scalar_tensor_tensor(lo, src, scale, hi, ALU.mult, ALU.subtract)

            sync(w0_in, 32)
            sync(w0_hi, 1)
            split_low(W0[:, 1, :, 0:D], STG0[:, 0], WS, W0[:, 0, :, 0:D]).then_inc(w0_lo, 1)
            sync(brow_hi, 1)
            split_low(brow[32:33, 0:D], b_row[0:1, 0:D], PR, brow[0:1, 0:D]).then_inc(brow_lo, 1)
            sync(w0_hi, 2)
            sync(brow_hi, 2)
            split_low(W0[:, 1, :, D:DC], PS[:, 7, 0:4 * H].rearrange("p (k c) -> p k c", k=K), WS,
                      W0[:, 0, :, D:DC]).then_inc(w0_lo, 1)
            sync(brow_hi, 2)
            split_low(brow[32:33, D:DC], PS[0:1, 7, 4 * H:6 * H], PR, brow[0:1, D:DC]).then_inc(brow_lo, 1)

            norm_vector(0, HN0, lambda e, t: e.wait_ge(x_in_s[t // TH], 16))
            for q in range(0, T // 2, 2):
                turn_copy(0, HT0, q)
            sync(feat_out, 2 * T)
            s_src = sv[:, :, 0:H].rearrange("p t h -> p h t")
            s_dst = sv[:, :, H:2 * H].rearrange("p t h -> p h t")
            v.reduce_max(cm[:, 0, :], s_dst, axis=AX.X).then_inc(cmax_l, 1)
            v.tensor_scalar(BIGS, s_dst, BIG, None, ALU.mult).then_inc(tabs, 1)
            v.tensor_scalar(NEGS, s_dst, -1.0, None, ALU.mult).then_inc(tabs, 1)
            sync(cmax, 1)
            top = cm[:, 1, :].unsqueeze(2).to_broadcast([P, H, T])
            v.tensor_tensor(SCR, s_dst, top, ALU.subtract).then_inc(tabs_d, 1)
            v.tensor_tensor(SCM, s_src, top, ALU.add).then_inc(tabs, 1)
            sync(tabs, 3)
            v.scalar_tensor_tensor(CB, SCM, 0.2, SCM, ALU.mult, ALU.max).then_inc(tabs_d, 1)
            sync(tabs_d, 2)
            v.tensor_tensor(CA, SCM, CB, ALU.subtract).then_inc(tabs, 1)
            sync(tabs, 4)
            v.scalar_tensor_tensor(CB, SCM, 0.2, CB, ALU.mult, ALU.subtract).then_inc(tabs, 1)
            for t in range(T):
                sync(ft_hi, t + 1)
                v.tensor_tensor(FT[:, :, t, :, 1, :], GR[:, t % 2], FT[:, :, t, :, 0, :], ALU.subtract)\
                    .then_inc(ft_lo, 1)
            for t in range(T):
                sync(cum_cp, 2 * t + 2)
                v.scalar_tensor_tensor(KT[:, t, :], CS[:, t % 2, :], CAP, AT[:, t, :], ALU.is_le, ALU.mult,
                                       saturate=False)\
                    .then_inc(kept, 1)
            sync(deg_mm, 1)
            v.tensor_scalar(deg[:, 0, :], PS[:, 4, 0:T], 1.0, None, ALU.mult).then_inc(deg_cp, 1)
            sync(deg_cp, 1)
            v.tensor_scalar(deg[:, 1, :], deg[:, 0, :], 1.0, PR, ALU.max, ALU.mult).then_inc(deg_rd, 1)
            v.tensor_scalar(deg[:, 2, :], deg[:, 0, :], 1.0, None, ALU.min).then_inc(deg_rd, 1)
            v.tensor_scalar(deg[:, 3, :], deg[:, 0, :], CAP, 1.0, ALU.min, ALU.max).then_inc(deg_rd, 1)
            sync(deg_rd, 3)
            v.reciprocal(deg[:, 4, :], deg[:, 1, :]).then_inc(deg_rd, 1)
            v.reciprocal(deg[:, 5, :], deg[:, 3, :]).then_inc(deg_rd, 1)
            sync(deg_rd, 5)
            v.tensor_scalar(deg[:, 5, :], deg[:, 5, :], 1.0 / PR, None, ALU.mult).then_inc(deg_rd, 1)
            sync(degb_cp, NC)

            def sums(h, half):
                n = h * 2 + half
                dve.wait_ge(lo_out, n + 1)
                if not (isinstance(h, int) and h == 0 and half == 0):
                    dve.wait_ge(t_used, n)
                hi = PS[:, 4 * half:4 * half + 4, :].rearrange("p b (i n) -> p (b i) n", i=2)[:, :, 0:6 * E]\
                    .rearrange("p t (g s c) -> p t g s c", g=3, s=2)[:, :, :, 0, :]
                v.tensor_tensor(TSUM, hi, TMP, ALU.add).then_inc(t_sum, 1)

            def shares(h, half):
                dve.wait_ge(mixed, h * 2 + half + 1)
                v.reciprocal(REC[:, :], TA[:, :, DH]).then_inc(share_out, 1)

            def head_vector(h, first):
                for half in range(2):
                    dve.wait_ge(sbc_in[half], h * 16 + 16)
                    n = 0
                    for t in range(T):
                        if t == 4 and not (first and half == 0):
                            sums(h - (half == 0), 1 - half)
                        if t == 9 and not (first and half == 0):
                            shares(h - (half == 0), 1 - half)
                        if not first or half * T + t >= NM:
                            dve.wait_ge(m_used, h * (2 * T) + half * T + t + 1 - NM)
                        adj = AT[:, t, half * HALF:(half + 1) * HALF]
                        if t in ALONE:
                            v.scalar_tensor_tensor(MS[:, t % NM, :], SBC[:, half, :],
                                                   NEGS[:, bass.ds(h, 1), t:t + 1].rearrange("p a t -> p (a t)"),
                                                   adj, ALU.is_gt, ALU.mult).then_inc(m_ready, 1)
                        else:
                            dve.wait_ge(y_ready, h * (2 * NYH) + half * NYH + n + 1)
                            v.tensor_tensor(MS[:, t % NM, :], YS[:, n % NY, :], adj, ALU.min)\
                                .then_inc(m_ready, 1)
                            n += 1

            head_vector(0, True)
            with dve.Fori(1, H) as h:
                head_vector(h, False)
            sums(H - 1, 1)
            shares(H - 1, 1)

            for m, wt in ((0, W1S), (1, W1Q)):
                sync(wc_hi, m + 1)
                split_low(wt[:, 1], PS[:, m, :].rearrange("p (k d) -> p k d", k=K), (WS, WQ)[m], wt[:, 0])\
                    .then_inc(wc_lo, 1)
            for m, wt in ((0, W2S), (1, W2Q)):
                sync(wc_hi, m + 3)
                split_low(wt[:, 1], STG1[:, 4 + m], (WS, WQ)[m], wt[:, 0]).then_inc(wc_lo, 1)
            sync(b1_mm, 1)
            v.tensor_tensor(b_row[:, 0:D], b_row[:, 0:D], PS[0:1, 2, 0:D], ALU.add).then_inc(b1_lo, 1)
            sync(b1_hi, 1)
            split_low(brow[32:33, 0:D], b_row[0:1, 0:D], PR, brow[0:1, 0:D]).then_inc(b1_lo, 1)

            def own_row(L):
                def wait(eng, t):
                    eng.wait_ge(x_heads if L == 1 else d_x[L - 1], 2 * H if L == 1 else t + 1)
                return wait

            for L in (1, 2):
                norm_vector(L, HN, own_row(L))
                for q in range(0, T // 2, 2):
                    turn_copy(L, HT, q)
                for n in range(K * NC):
                    sum_vector(n, q_mm[L], q_hi[L], q_lo[L], 0)

                def value(t):
                    sync(d_mm[L], t + 1)
                    sync(d_sf[L], t + 1)
                    if L == 2:
                        v.scalar_tensor_tensor(SF[:, t % 2, :], SF[:, t % 2, :], 0.01, SF[:, t % 2, :],
                                               ALU.mult, ALU.max).then_inc(d_xi, 1)
                    if t >= 2:
                        sync(d_x[L], t - 1)
                    v.scalar_tensor_tensor(SV2[:, t % 2, :], PS[:, t % 2, D:2 * D], deg[:, 3 + L, t:t + 1],
                                           SF[:, t % 2, :] if L == 1 else bn_bc[:, :], ALU.mult, ALU.add)\
                        .then_inc(d_v[L], 1)

                def join(t):
                    sync(d_v[L], t + 1)
                    if L == 1:
                        v.scalar_tensor_tensor(X[:, t, :], SV2[:, t % 2, :], 0.0, X[:, t, :], ALU.max, ALU.add)\
                            .then_inc(d_x[1], 1)
                    else:
                        v.scalar_tensor_tensor(SV2[:, t % 2, :], SV2[:, t % 2, :], 0.01, SV2[:, t % 2, :],
                                               ALU.mult, ALU.max).then_inc(d_lr, 1)
                        sync(d_lr, t + 1)
                        sync(d_u[2], t + 1)
                        v.scalar_tensor_tensor(X[:, t, :], SV2[:, t % 2, :], deg[:, 2, t:t + 1], X[:, t, :],
                                               ALU.mult, ALU.add).then_inc(d_x[2], 1)

                for t in range(T):
                    value(t)
                    if t >= 1:
                        join(t - 1)
                join(T - 1)
                if L == 1:
                    sync(b2_hi, 1)
                    split_low(brow[32:33, 0:D], b_row[0:1, 0:D], PR, brow[0:1, 0:D]).then_inc(b2_lo, 1)

            for g in range(3):
                sync(w3_hi, g + 1)
                split_low(WQG[g][:, 1], PS[:, g, :].rearrange("p (k d) -> p k d", k=K), WQ, WQG[g][:, 0])\
                    .then_inc(w3_lo, 1)
            for g in range(3):
                sync(w3_hi, g + 4)
                split_low(WSG[g][:, 1], STG3[:, 4 + 3 * g], WS, WSG[g][:, 0]).then_inc(w3_lo, 1)
            for n, (m, wt) in enumerate(((11, WO1), (12, WO2))):
                sync(w3_hi, n + 7)
                split_low(wt[:, 1], STG3[:, m], WS, wt[:, 0]).then_inc(w3_lo, 1)
            sync(bo_hi, 1)
            split_low(brow[32:33, 0:D], b_row[0:1, 0:D], PR, brow[0:1, 0:D]).then_inc(bo_lo, 1)
            norm_vector(3, HN, own_row(3))
            for q in range(0, T // 2, 2):
                turn_copy(3, HT, q)
            sync(x_out, 16)

            def sums_of_step(step):
                for n in range(K * NC):
                    sum_vector(n, q_mm[0], q_hi[0], q_lo[0], step * (K * NC))

            def gates_vector(step):
                def old(k2, c):
                    if c >= 3:
                        sync(new_f, step * (K * NC) + K * (c - 3) + k2 + 1)
                    v.tensor_tensor(SG[:, c % 3, k2, :], HT[:, 0, k2, c * CH:(c + 1) * CH],
                                    HT[:, 1, k2, c * CH:(c + 1) * CH], ALU.add).then_inc(st_r, 1)

                def bias(gate, c, mm_sem, mm_base, done):
                    for k2 in range(K):
                        bank = gate * K + k2
                        sync(mm_sem, mm_base + k2 + 1)
                        v.scalar_tensor_tensor(PS[:, bank, :], degb[:, c * CH:(c + 1) * CH],
                                               vcol[:, bank:bank + 1], PS[:, bank, :], ALU.mult, ALU.add)\
                            .then_inc(done, 1)

                def reset(c):
                    bias(0, c, rz_mm, step * (4 * NC) + 4 * c, rz_deg)
                    for k2 in range(K):
                        old(k2, c)
                    for k2 in range(K):
                        sync(st_r, step * (K * NC) + K * c + k2 + 1)
                        sync(rz_act, step * (4 * NC) + 4 * c + k2 + 1)
                        v.tensor_tensor(RG[:, k2, :], RG[:, k2, :], SG[:, c % 3, k2, :], ALU.mult).then_inc(rs_f, 1)
                    bias(1, c, rz_mm, step * (4 * NC) + 4 * c + K, rz_deg)
                    for k2 in range(K):
                        sync(rs_hi, step * (K * NC) + K * c + k2 + 1)
                        v.tensor_tensor(RSB[:, c % 2, 1, k2, :], RG[:, k2, :], RSB[:, c % 2, 0, k2, :],
                                        ALU.subtract).then_inc(rs_lo, 1)

                def update(c):
                    base = step * (K * NC) + K * c
                    bias(2, c, h_mm, base, h_deg)
                    for k2 in range(K):
                        sync(h_act, base + k2 + 1)
                        v.scalar_tensor_tensor(HG[:, k2, :], HG[:, k2, :], ST, SG[:, c % 3, k2, :], ALU.mult,
                                               ALU.subtract).then_inc(up_a, 1)
                    for k2 in range(K):
                        sync(up_a, base + k2 + 1)
                        sync(rz_act, step * (4 * NC) + 4 * c + K + k2 + 1)
                        v.tensor_tensor(HG[:, k2, :], HG[:, k2, :], ZR[:, c % 2, k2, :], ALU.mult)\
                            .then_inc(up_b, 1)
                    for k2 in range(K):
                        sync(up_b, base + k2 + 1)
                        v.tensor_tensor(HG[:, k2, :], HG[:, k2, :], SG[:, c % 3, k2, :], ALU.add).then_inc(new_f, 1)
                    for k2 in range(K):
                        sync(new_hi, base + k2 + 1)
                        v.tensor_tensor(HT[:, 1, k2, c * CH:(c + 1) * CH], HG[:, k2, :],
                                        HT[:, 0, k2, c * CH:(c + 1) * CH], ALU.subtract).then_inc(new_lo, 1)

                reset(0)
                reset(1)
                update(0)
                reset(2)
                update(1)
                reset(3)
                update(2)
                update(3)

            sync(state_c, 1)
            sums_of_step(0)
            with dve.Fori(0, STEPS - 1) as step:
                gates_vector(step)
                sums_of_step(step + 1)
            gates_vector(STEPS - 1)

            for n in range(K * NC):
                c, k2 = n // K, n % K
                sync(o1_hi, n + 1)
                v.scalar_tensor_tensor(QT[:, 1, k2, c * CH:(c + 1) * CH], HG[:, n % 2, :], ST,
                                       QT[:, 0, k2, c * CH:(c + 1) * CH], ALU.mult, ALU.subtract)\
                    .then_inc(o1_lo, 1)
            sync(x_back, 16)
            for t in range(T):
                sync(o2_mm, t + 1)
                v.scalar_tensor_tensor(OB[:, t, :], PS[:, t % 2, 0:D], 1.0 / PR, XF[:, t, :], ALU.mult, ALU.add)\
                    .then_inc(o2_x, 1)


def kernel(x, adj, L0_gnn_W_w, L0_gnn_W_b, L0_gnn_a, L1_gnn_W_self, L1_gnn_b_self, L1_gnn_W_nb, L1_gnn_b_nb,
           L1_gnn_W_comb, L1_gnn_b_comb, L2_gnn_W_nb, L2_gnn_b_nb, L2_gnn_W_line, L2_gnn_b_line, L3_gnn_in_W,
           L3_gnn_in_b, L3_gnn_out_W, L3_gnn_out_b, L3_gnn_r_W, L3_gnn_r_b, L3_gnn_z_W, L3_gnn_z_b, L3_gnn_h_W,
           L3_gnn_h_b, L3_gnn_o1_W, L3_gnn_o1_b, L3_gnn_o2_W, L3_gnn_o2_b):
    import concourse.bacc as bacc
    from concourse.bass_utils import run_bass_kernel_spmd

    arr = np.asarray
    D = x.shape[1]
    data = {
        "x": arr(x), "adj_t": arr(adj).T, "l0_w": arr(L0_gnn_W_w), "l0_wt": arr(L0_gnn_W_w).T,
        "l0_b": arr(L0_gnn_W_b), "l0_a": arr(L0_gnn_a),
        "l1_ws_t": arr(L1_gnn_W_self).T, "l1_wn_t": arr(L1_gnn_W_nb).T,
        "l1_wc1": arr(L1_gnn_W_comb)[:D], "l1_wc2": arr(L1_gnn_W_comb)[D:],
        "l1_bs": arr(L1_gnn_b_self), "l1_bn": arr(L1_gnn_b_nb), "l1_bc": arr(L1_gnn_b_comb),
        "l2_wl_t": arr(L2_gnn_W_line).T, "l2_wn_t": arr(L2_gnn_W_nb).T,
        "l2_bl": arr(L2_gnn_b_line), "l2_bn": arr(L2_gnn_b_nb),
        "l3_in_w": arr(L3_gnn_in_W), "l3_out_w": arr(L3_gnn_out_W),
        "l3_in_b": arr(L3_gnn_in_b), "l3_out_b": arr(L3_gnn_out_b),
        "l3_rb": arr(L3_gnn_r_b), "l3_zb": arr(L3_gnn_z_b), "l3_hb": arr(L3_gnn_h_b),
        "l3_o1_t": arr(L3_gnn_o1_W).T, "l3_o1b": arr(L3_gnn_o1_b),
        "l3_o2_t": arr(L3_gnn_o2_W).T, "l3_o2b": arr(L3_gnn_o2_b),
    }
    for g, wg in (("r", L3_gnn_r_W), ("z", L3_gnn_z_W), ("h", L3_gnn_h_W)):
        for n in range(3):
            data[f"l3_{g}_t{n}"] = arr(wg)[:, n * D:(n + 1) * D].T

    for name in ("l0_b", "l1_bs", "l1_bn", "l3_in_b", "l3_out_b", "l3_rb", "l3_zb", "l3_hb", "l3_o1b"):
        data[name + "_c"] = data[name].reshape(-1, 128).T

    nc = bacc.Bacc("TRN2", target_bir_lowering=False, num_devices=1)
    arrays, aps = {}, {}
    for name, a in data.items():
        a = np.ascontiguousarray(a)
        arrays[f"in_{name}"] = a
        aps[name] = nc.dram_tensor(f"in_{name}", a.shape, mybir.dt.from_np(a.dtype), kind="ExternalInput").ap()
    out = nc.dram_tensor("out", x.shape, mybir.dt.float32, kind="ExternalOutput").ap()
    gnn_stack_kernel(nc, aps.pop("x"), aps.pop("adj_t"), aps, out)
    r = run_bass_kernel_spmd(nc, [arrays], core_ids=[0])
    return r.results[0]["out"]
```

```python
import numpy as np
import concourse.bass as bass
from concourse import mybir
from contextlib import ExitStack


def gnn_stack_kernel(nc, x_in, adj_t, w, out):
    F32, F16, BF16, F8, U8 = (mybir.dt.float32, mybir.dt.float16, mybir.dt.bfloat16, mybir.dt.float8e4,
                              mybir.dt.uint8)
    ALU = mybir.AluOpType
    ACT = mybir.ActivationFunctionType
    AX = mybir.AxisListType
    RMAX = bass.bass_isa.ReduceOp.max

    P = 128
    N, D = x_in.shape
    T = N // P
    K = D // P
    H = 8
    DH = D // H
    E = DH + 1
    CH = 512
    NC = N // CH
    HALF = N // 2
    TH = T // 2
    CAP = 64.0
    STEPS = 5
    ST, WS, WQ = 16.0, 64.0, 1024.0
    PR = ST * WS
    UP = 8.0 * float(np.log(2.0))
    BIG = float(2.0 ** 60)
    EPS = 1e-5
    DC = D + 2 * H
    KB = K * D * 2 * 2

    ctx = ExitStack()
    with ctx:
        def sem(name):
            return ctx.enter_context(nc.semaphore(name))

        def sb(name, shape, dt):
            return ctx.enter_context(nc.sbuf_tensor(name, shape, dt))

        ARENA = 202752
        arena = sb("arena", [P, ARENA], U8)

        def at(off, n, dt):
            size = {F32: 4, F16: 2, BF16: 2, F8: 1}[dt]
            assert off % 4 == 0 and off + n * size <= ARENA
            return arena[:, off:off + n * size].bitcast(dt)

        AT_O = 0
        KD_O = AT_O + T * N * 2
        HN_O = KD_O + T * N
        HT_O = HN_O + 2 * T * D * 2
        Q_O = HT_O + 2 * T * D * 2
        DQ_O = Q_O + 2 * T * D * 2
        X_O = DQ_O + 2 * T * D * 2
        WA_O = X_O + T * D * 4

        AT = at(AT_O, T * N, BF16).rearrange("p (t n) -> p t n", t=T)
        KT = at(KD_O, T * N, F8).rearrange("p (t n) -> p t n", t=T)
        HN = at(HN_O, 2 * T * D, F16).rearrange("p (t s d) -> p t s d", t=T, s=2)
        HT = at(HT_O, 2 * T * D, F16).rearrange("p (s k n) -> p s k n", s=2, k=K)
        QT = at(Q_O, 2 * T * D, F16).rearrange("p (s k n) -> p s k n", s=2, k=K)
        X = at(X_O, T * D, F32).rearrange("p (t d) -> p t d", t=T)

        HT0 = at(HN_O, 2 * T * D, F16).rearrange("p (s k n) -> p s k n", s=2, k=K)
        HN0 = at(HT_O, 2 * T * D, F16).rearrange("p (t s d) -> p t s d", t=T, s=2)
        FTW = 4 * E
        FTF = at(HN_O, H * T * FTW, F16)
        FT = FTF.rearrange("p (h t e s c) -> p h t e s c", h=H, t=T, e=2, s=2)
        SBC_O = HN_O + H * T * FTW * 2
        SBC = at(SBC_O, 2 * HALF, F32).rearrange("p (b n) -> p b n", b=2)
        MS_O = SBC_O + 2 * HALF * 4
        NM = 8
        MS = at(MS_O, NM * HALF, BF16).rearrange("p (b n) -> p b n", b=NM)
        NY = 3
        YS_O = MS_O + NM * HALF * 2
        YS = at(YS_O, NY * HALF, BF16).rearrange("p (b n) -> p b n", b=NY)
        assert YS_O + NY * HALF * 2 <= X_O
        STG0 = at(KD_O, 2 * K * D, F32).rearrange("p (m k d) -> p m k d", m=2, k=K)
        SROW = at(SBC_O, N, F32)
        CS_O = WA_O + 2 * K * DC * 2
        CS = at(CS_O, 2 * N, F16).rearrange("p (b n) -> p b n", b=2)
        HF_O = MS_O
        HF = at(HF_O, T * H * E, F32).rearrange("p (t h c) -> p t h c", t=T, h=H)
        GR_O = HF_O + T * H * E * 4
        SV_O = GR_O + 2 * H * 2 * E * 4
        assert SV_O + T * 2 * H * 4 <= X_O
        GR = at(GR_O, 2 * H * 2 * E, F32).rearrange("p (b h e c) -> p b h e c", b=2, h=H, e=2)
        W0 = at(WA_O, 2 * K * DC, F16).rearrange("p (s k d) -> p s k d", s=2, k=K)
        TM_O = WA_O + 2 * K * DC * 2
        TSZ = TH * 3 * E
        TMP = at(TM_O, TSZ, F32).rearrange("p (t g c) -> p t g c", t=TH, g=3)
        TSUM = at(TM_O + TSZ * 4, TSZ, F32).rearrange("p (t g c) -> p t g c", t=TH, g=3)
        TA = at(TM_O + 2 * TSZ * 4, TH * E, F32).rearrange("p (t c) -> p t c", t=TH)
        TB = at(TM_O + 2 * TSZ * 4 + TH * E * 4, TH * E, F32).rearrange("p (t c) -> p t c", t=TH)
        TV_O = TM_O + 2 * TSZ * 4 + 2 * TH * E * 4
        TV, TN, TE = (at(TV_O + n * TH * DH * 4, TH * DH, F32).rearrange("p (t c) -> p t c", t=TH)
                      for n in range(3))
        TP = at(YS_O + NY * HALF * 2, TH * DH, F32).rearrange("p (t c) -> p t c", t=TH)
        assert YS_O + NY * HALF * 2 + TH * DH * 4 <= X_O
        REC = at(TV_O + 3 * TH * DH * 4, TH, F32)

        def weight(n):
            return at(WA_O + n * KB, 2 * K * D, F16).rearrange("p (s k d) -> p s k d", s=2, k=K)

        W1S, W1Q, W2S, W2Q = (weight(n) for n in range(7, 11))
        assert TV_O + 3 * TH * DH * 4 + TH * 4 <= WA_O + 7 * KB
        STG1_O = KD_O + T * N - 6 * K * D * 4
        STG1 = at(STG1_O, 6 * K * D, F32).rearrange("p (m k d) -> p m k d", m=6, k=K)
        SF_O = DQ_O + 6 * K * D * 4
        SF = at(SF_O, 2 * D, F32).rearrange("p (b d) -> p b d", b=2)
        SV2 = at(SF_O + 2 * D * 4, 2 * D, F32).rearrange("p (b d) -> p b d", b=2)
        SF01 = at(DQ_O + 3 * K * D * 4, 2 * D, F32).rearrange("p (b d) -> p b d", b=2)
        STG3 = at(DQ_O, 6 * K * D, F32).rearrange("p (m k d) -> p m k d", m=6, k=K)
        WQG = [weight(n) for n in range(3)]
        WSG = [weight(n) for n in range(3, 6)]
        WO1, WO2 = weight(6), weight(7)
        ZR = at(X_O, 2 * K * CH, F32).rearrange("p (b k n) -> p b k n", b=2, k=K)
        RSB = at(X_O + 2 * K * CH * 4, 2 * 2 * K * CH, F16).rearrange("p (b s k n) -> p b s k n", b=2, s=2, k=K)
        RG = at(DQ_O, 2 * CH, F32).rearrange("p (b n) -> p b n", b=2)
        SG = at(KD_O + T * D * 4, 3 * K * CH, F32).rearrange("p (b k n) -> p b k n", b=3, k=K)
        HG = at(DQ_O + 8192, 2 * CH, F32).rearrange("p (b n) -> p b n", b=2)
        XF = at(KD_O, T * D, F32).rearrange("p (t d) -> p t d", t=T)
        OB = at(KD_O + T * D * 4, T * D, F32).rearrange("p (t d) -> p t d", t=T)

        ident = sb("ident", [P, P], F16)
        tri = sb("tri", [P, P], BF16)
        last_row = sb("last_row", [P, P], F16)
        ones = sb("ones", [P, P], F16)
        share = sb("share", [P, 2], F16)
        eps_c = sb("eps_c", [P, 1], F32)
        up_c = sb("up_c", [P, 1], F32)
        a_sel = sb("a_sel", [P, K, 2 * H], F32)
        b_col = sb("b_col", [P, 8 * K], F32)
        b_row = sb("b_row", [P, D], F32)
        bn_bc = b_row
        brow = sb("brow", [P, DC], F16)
        vcol = sb("vcol", [P, 3 * K], F32)
        degb = sb("degb", [P, N], F16)
        stats = sb("stats", [P, 4, 6], F32)
        mv = sb("mv", [P, T, 2], F32)
        rstd = sb("rstd", [P, T], F32)
        nmr = sb("nmr", [P, T], F32)
        deg = sb("deg", [P, 6, T], F32)
        tb = sb("tb", [P, 4, H, T], F32)
        ts_ = at(CS_O + 2 * N * 2, 4 * H * T, F32).rearrange("p (n h t) -> p n h t", n=4, h=H)
        cm = sb("cm", [P, 2, H], F32)
        sv = at(SV_O, T * 2 * H, F32).rearrange("p (t c) -> p t c", t=T)
        HSC = tb.rearrange("p n h t -> p (n h t)").rearrange("p (b d) -> p b d", b=2)
        BIGS, NEGS, CA, CB = (tb[:, n] for n in range(4))
        E1, E2, SCR, SCM = (ts_[:, n] for n in range(4))

        PS = ctx.enter_context(nc.psum_tensor("ps", [P, 8, CH], F32))
        PS16 = [PS[:, b, :].bitcast(F16) for b in range(8)]

        bigs = sb("bigs", [P, 2, T], F32)
        bigs_in = sem("bigs_in")
        s_dram = nc.dram_tensor("source_scores", [H, N], F32, kind="Internal").ap()
        x_dram = nc.dram_tensor("residual", [N, D], F32, kind="Internal").ap()
        rows = "(t p) d -> p t d"

        consts = sem("consts")
        at_in = [sem(f"at_in{t}") for t in range(T // 2)]
        x_in_s = [sem(f"x_in{t}") for t in range(2)]
        w0_in, asel_in, asel_zero, b0_in = sem("w0_in"), sem("asel_in"), sem("asel_zero"), sem("b0_in")
        fold0, w0_hi, w0_lo = sem("fold0"), sem("w0_hi"), sem("w0_lo")
        brow_hi, brow_lo, brow_zero = sem("brow_hi"), sem("brow_lo"), sem("brow_zero")
        pool_c = sem("pool_c")
        NG = T // 4
        per_layer = {"var": T, "norm": T, "std": NG, "inv": 2 * NG, "h_pre": T, "h_hi": T, "h_lo": T, "turned": T // 2,
                     "turn_a": T // 4, "turn_v": T // 4}
        ls = {k: sem(k) for k in per_layer}

        def wait_layer(eng, L, k, n):
            eng.wait_ge(ls[k], L * per_layer[k] + n)

        feat, feat_out, srow_mm, srow_out, srow_st = (sem("feat"), sem("feat_out"), sem("srow_mm"),
                                                      sem("srow_out"), sem("srow_st"))
        cmax_l, cmax, tabs_d, tabs_e, tabs = (sem("cmax_l"), sem("cmax"), sem("tabs_d"), sem("tabs_e"), sem("tabs"))
        g_done, ft_hi, ft_lo = sem("g_done"), sem("ft_hi"), sem("ft_lo")
        cum_mm, cum_cp, kept = sem("cum_mm"), sem("cum_cp"), sem("kept")
        degb_mm, degb_cp, deg_mm, deg_cp, deg_rd = (sem("degb_mm"), sem("degb_cp"), sem("deg_mm"),
                                                    sem("deg_cp"), sem("deg_rd"))
        sbc_in = [sem("sbc_in0"), sem("sbc_in1")]
        y_ready, m_ready, m_used = sem("y_ready"), sem("m_ready"), sem("m_used")
        lo_out, t_sum, t_used, share_out = sem("lo_out"), sem("t_sum"), sem("t_used"), sem("share_out")
        mix_a, mixed, divided, neg_ready, pos_ready, exp_ready, pos_added, x_heads = (sem(n) for n in (
            "mix_a", "mixed", "divided", "neg_ready", "pos_ready", "exp_ready", "pos_added", "x_heads"))
        w1_in, wc_mm, wc_hi, wc_lo = sem("w1_in"), sem("wc_mm"), sem("wc_hi"), sem("wc_lo")
        b1_mm, b1_hi, b1_lo, b1_in = sem("b1_mm"), sem("b1_hi"), sem("b1_lo"), sem("b1_in")
        q_mm = [sem(f"q_mm{n}") for n in range(3)]
        q_hi = [sem(f"q_hi{n}") for n in range(3)]
        q_lo = [sem(f"q_lo{n}") for n in range(3)]
        d_mm = [sem(f"d_mm{n}") for n in range(3)]
        d_sf = [sem(f"d_sf{n}") for n in range(3)]
        d_v = [sem(f"d_v{n}") for n in range(3)]
        d_x = [sem(f"d_x{n}") for n in range(3)]
        d_u = [sem(f"d_u{n}") for n in range(3)]
        b2_hi, b2_lo, d_xi, d_lr, up_a, up_b = sem("b2_hi"), sem("b2_lo"), sem("d_xi"), sem("d_lr"), sem("up_a"), sem("up_b")
        x_out, x_back = sem("x_out"), sem("x_back")
        w3_hi, w3_lo = sem("w3_hi"), sem("w3_lo")
        w3_in = [sem(f"w3_in{n}") for n in range(3)]
        v_mm, v_hi = sem("v_mm"), sem("v_hi")
        d_own = sem("d_own")
        rz_deg, h_deg = sem("rz_deg"), sem("h_deg")
        rz_mm, rz_act, st_r, rs_f, rs_hi, rs_lo, h_mm, h_act = (sem(n) for n in (
            "rz_mm", "rz_act", "st_r", "rs_f", "rs_hi", "rs_lo", "h_mm", "h_act"))
        new_f, new_hi, new_lo, back_mm, back_cp = (sem(n) for n in (
            "new_f", "new_hi", "new_lo", "back_mm", "back_cp"))
        o1_mm, o1_act, o1_hi, o1_lo, o2_mm, o2_x, o2_out, row_in, bo_hi, bo_lo = (sem(n) for n in (
            "o1_mm", "o1_act", "o1_hi", "o1_lo", "o2_mm", "o2_x", "o2_out", "row_in", "bo_hi", "bo_lo"))

        PARTS = ((0, 0), (0, 1), (1, 0))
        block = ctx.enter_context(nc.Block())

        def mat(a):
            return a.rearrange("(k p) d -> p k d", p=P)

        ALONE = (2, 6, 10, 14)
        STARTED = [t for t in range(T) if t not in ALONE]
        NYH = len(STARTED)
        assert NYH % NY == 0 and T % NM == 0

        @block.sync
        def _(sp):
            x_v = x_in.rearrange(rows, p=P)
            for n in range(2):
                sp.dma_start(X[:, n * TH:(n + 1) * TH, :], x_v[:, n * TH:(n + 1) * TH, :]).then_inc(x_in_s[n], 16)
            sp.dma_start(STG0[:, 0], mat(w["l0_wt"])).then_inc(w0_in, 16)
            sp.dma_start(STG0[:, 1], mat(w["l0_w"])).then_inc(w0_in, 16)
            sp.dma_start(b_row[0:1, 0:D], w["l0_b"].rearrange("(a n) -> a n", a=1)).then_inc(b0_in, 16)
            sp.dma_start(b_col[:, 0:K], w["l0_b_c"]).then_inc(b0_in, 16)
            sp.wait_ge(asel_zero, 1)
            for h in range(H):
                for side in range(2):
                    sp.dma_start(a_sel[h % 4 * DH:(h % 4 + 1) * DH, h // 4, side * H + h:side * H + h + 1],
                                 w["l0_a"][side * DH:(side + 1) * DH, :]).then_inc(asel_in, 16)
            for n, name in enumerate(("l1_ws_t", "l1_wn_t", "l1_wc1", "l1_wc2", "l2_wl_t", "l2_wn_t")):
                sp.dma_start(STG1[:, n], mat(w[name])).then_inc(w1_in, 16)
            sp.dma_start(b_col[:, K:2 * K], w["l1_bs_c"]).then_inc(b1_in, 16)
            sp.dma_start(b_col[:, 2 * K:3 * K], w["l1_bn_c"]).then_inc(b1_in, 16)
            sp.wait_ge(brow_hi, 1)
            sp.wait_ge(brow_lo, 1)
            sp.dma_start(b_row[0:1, 0:D], w["l1_bc"].rearrange("(a n) -> a n", a=1)).then_inc(row_in, 16)
            sp.wait_ge(srow_out, NC)
            sp.dma_start(s_dram[:, :], SROW[0:H, :]).then_inc(srow_st, 16)
            sp.wait_ge(srow_st, 16)

            def scores_of(h, b):
                sp.dma_start(SBC[:, b, :], s_dram[bass.ds(h, 1), b * HALF:(b + 1) * HALF]
                             .to_broadcast([P, HALF])).then_inc(sbc_in[b], 16)

            for b in range(2):
                scores_of(0, b)
            with sp.Fori(1, H) as h:
                for b in range(2):
                    sp.wait_ge(m_ready, h * (2 * T) + (b + 1) * T - 2 * T)
                    scores_of(h, b)
            sp.wait_ge(m_used, 2 * H * T)
            sp.wait_ge(x_heads, 2 * H)
            for n, name in enumerate(("l3_r_t2", "l3_z_t2", "l3_h_t2", "l3_o1_t", "l3_in_w", "l3_out_w")):
                sp.dma_start(STG3[:, n], mat(w[name])).then_inc(w3_in[0], 16)
            for n, name in enumerate(("l3_in_b", "l3_out_b", "l3_rb", "l3_zb", "l3_hb", "l3_o1b")):
                sp.dma_start(b_col[:, (n + 2) * K if n > 1 else n * K:(n + 3) * K if n > 1 else (n + 1) * K],
                             w[name + "_c"]).then_inc(w3_in[0], 16)
            sp.wait_ge(b1_hi, 1)
            sp.wait_ge(b1_lo, 2)
            sp.dma_start(b_row[0:1, 0:D], w["l2_bl"].rearrange("(a n) -> a n", a=1)).then_inc(row_in, 16)
            sp.wait_ge(w3_hi, 4)
            sp.wait_ge(w3_lo, 4)
            for n, name in enumerate(("l3_r_t0", "l3_r_t1", "l3_z_t0", "l3_z_t1")):
                sp.dma_start(STG3[:, n], mat(w[name])).then_inc(w3_in[1], 16)
            sp.wait_ge(v_mm, 2)
            for n, name in enumerate(("l3_h_t0", "l3_h_t1", "l3_o2_t")):
                sp.dma_start(STG3[:, n], mat(w[name])).then_inc(w3_in[2], 16)
            sp.wait_ge(b2_hi, 1)
            sp.wait_ge(b2_lo, 1)
            sp.dma_start(bn_bc[:, :], w["l2_bn"].rearrange("(a n) -> a n", a=1).to_broadcast([P, D]))\
                .then_inc(row_in, 16)
            sp.wait_ge(d_x[2], T)
            sp.dma_start(x_dram.rearrange(rows, p=P), X).then_inc(x_out, 16)
            sp.wait_ge(q_mm[2], K * NC)
            sp.wait_ge(d_v[2], T)
            sp.dma_start(b_row[0:1, 0:D], w["l3_o2b"].rearrange("(a n) -> a n", a=1)).then_inc(row_in, 16)
            sp.wait_ge(x_out, 16)
            sp.dma_start(XF, x_dram.rearrange(rows, p=P)).then_inc(x_back, 16)
            out_v = out.rearrange(rows, p=P)
            for t in range(T // 2):
                sp.wait_ge(o2_x, 2 * t + 2)
                sp.dma_start(out_v[:, 2 * t:2 * t + 2, :], OB[:, 2 * t:2 * t + 2, :]).then_inc(o2_out, 16)
            sp.wait_ge(o2_out, 16 * (T // 2))

        @block.gpsimd
        def _(pool):
            g = nc.gpsimd
            g.memset(a_sel[:, :, :], 0.0).then_inc(asel_zero, 1)
            g.memset(ones[:, :], 1.0).then_inc(pool_c, 1)
            g.memset(tri[:, :], 1.0).then_inc(pool_c, 1)
            g.memset(share[:, :], 1.0 / P).then_inc(pool_c, 1)
            g.memset(eps_c[:, :], EPS / ST ** 2).then_inc(pool_c, 1)
            g.memset(up_c[:, :], UP).then_inc(pool_c, 1)
            g.memset(brow[:, :], 0.0).then_inc(brow_zero, 1)
            pool.wait_ge(pool_c, 5)
            g.affine_select(out=ident[:, :], in_=ones[:, :], compare_op=ALU.is_equal, fill=0.0, base=0,
                            pattern=[[-1, P]], channel_multiplier=1).then_inc(consts, 1)
            g.affine_select(out=tri[:, :], in_=tri[:, :], compare_op=ALU.is_ge, fill=0.0, base=0,
                            pattern=[[1, P]], channel_multiplier=-1).then_inc(consts, 1)
            g.affine_select(out=last_row[:, :], in_=ones[:, :], compare_op=ALU.is_ge, fill=0.0, base=1 - P,
                            pattern=[[0, P]], channel_multiplier=1).then_inc(consts, 1)
            g.memset(HF[:, :, :, DH:E], 1.0).then_inc(consts, 1)
            pool.wait_ge(x_in_s[0], 16)
            pool.wait_ge(x_in_s[1], 16)
            pool.wait_ge(w0_in, 32)
            for t in range(T):
                g.dma_start(AT[:, t, :], adj_t[t * P:(t + 1) * P, :]).then_inc(at_in[t // 2], 16)
            pool.wait_ge(cmax_l, 1)
            g.partition_all_reduce(cm[:, 1, :], cm[:, 0, :], P, RMAX).then_inc(cmax, 1)
            pool.wait_ge(tabs_e, 4)
            pool.wait_ge(feat_out, 2 * T)
            for t in range(T):
                if t >= 2:
                    pool.wait_ge(ft_lo, t - 1)
                for e, tab in ((0, E1), (1, E2)):
                    g.tensor_tensor(GR[:, t % 2, :, e, :], HF[:, t, :, :],
                                    tab[:, :, t:t + 1].to_broadcast([P, H, E]), ALU.mult).then_inc(g_done, 1)

            pool.wait_ge(ft_lo, T)

            def finish(h, half):
                lo = half * TH
                n = h * 2 + half + 1

                def per_source(tab, width):
                    return tab[:, bass.ds(h, 1), lo:lo + TH].rearrange("p a t -> p (a t)").unsqueeze(2)\
                        .to_broadcast([P, TH, width])

                pool.wait_ge(t_sum, n)
                g.tensor_tensor(TB, TSUM[:, :, 2, :], TSUM[:, :, 1, :], ALU.subtract).then_inc(mix_a, 1)
                g.tensor_tensor(TA, TSUM[:, :, 0, :], per_source(CA, E), ALU.mult).then_inc(mix_a, 1)
                pool.wait_ge(mix_a, 2 * n)
                g.tensor_tensor(TB, TB, per_source(CB, E), ALU.mult).then_inc(t_used, 1)
                pool.wait_ge(t_used, n)
                g.tensor_tensor(TA, TA, TB, ALU.add).then_inc(mixed, 1)
                pool.wait_ge(mixed, n)
                pool.wait_ge(share_out, n)
                g.tensor_tensor(TV, TA[:, :, 0:DH], REC[:, :].unsqueeze(2).to_broadcast([P, TH, DH]), ALU.mult)\
                    .then_inc(divided, 1)
                pool.wait_ge(divided, n)
                g.tensor_scalar(TN, TV, 0.0, None, ALU.min).then_inc(neg_ready, 1)
                g.tensor_scalar(TP, TV, 0.0, -1.0, ALU.max, ALU.add).then_inc(pos_ready, 1)
                pool.wait_ge(pos_ready, n)
                xs = X[:, lo:lo + TH, bass.ds(h * DH, DH)]
                g.tensor_tensor(xs, xs, TP, ALU.add).then_inc(pos_added, 1)
                pool.wait_ge(pos_added, n)
                pool.wait_ge(exp_ready, n)
                g.tensor_tensor(xs, xs, TE, ALU.add).then_inc(x_heads, 1)

            for n in range(2 * H - 1):
                finish(n // 2, n % 2)
            for t in range(T):
                pool.wait_ge(d_xi, t + 1)
                pool.wait_ge(d_sf[2], t + 1)
                g.tensor_tensor(SF[:, t % 2, :], SF[:, t % 2, :], SF01[:, t % 2, :], ALU.add)\
                    .then_inc(d_own, 1)
                pool.wait_ge(d_own, t + 1)
                g.tensor_tensor(X[:, t, :], X[:, t, :], SF[:, t % 2, :], ALU.add).then_inc(d_u[2], 1)

        LN_BEGUN = 6
        W0_AT = 12
        BANK = (0, 1, 7)
        LN_STEPS = T + 13

        def norm_vector(L, hn, ht, i, x_wait):
            v = nc.vector
            if 0 <= i - 2 < T:
                wait_layer(v, L, "var", i - 1)
                v.bn_aggr(mv[:, i - 2, :], stats[:, (i - 2) % 4, :]).then_inc(ls["norm"], 1)
            if 0 <= i - 1 < T:
                x_wait(v, i - 1)
                if i - 1 >= 4:
                    wait_layer(v, L, "norm", i - 4)
                v.bn_stats(stats[:, (i - 1) % 4, :], X[:, i - 1, :]).then_inc(ls["var"], 1)
            if i >= 7 and (i - 7) % 4 == 0 and i - 7 < T:
                g = (i - 7) // 4
                cols = slice(4 * g, 4 * g + 4)
                wait_layer(v, L, "std", g + 1)
                v.reciprocal(rstd[:, cols], nmr[:, cols]).then_inc(ls["inv"], 1)
                wait_layer(v, L, "inv", 2 * g + 1)
                v.scalar_tensor_tensor(nmr[:, cols], mv[:, cols, 0], -1.0, rstd[:, cols], ALU.mult, ALU.mult)\
                    .then_inc(ls["inv"], 1)
            if 0 <= i - 9 < T:
                t = i - 9
                wait_layer(v, L, "h_hi", t + 1)
                v.tensor_tensor(hn[:, t, 1, :], HSC[:, t % 2, :], hn[:, t, 0, :], ALU.subtract)\
                    .then_inc(ls["h_lo"], 1)
            if i >= 14 and (i - 14) % 4 == 0 and i - 14 < T:
                turn_copy(L, ht, (i - 14) // 2)

        def norm_scalar(L, hn, ht, i):
            if i >= 6 and (i - 6) % 4 == 0 and i - 6 < T:
                cols = slice(i - 6, i - 2)
                wait_layer(nc.scalar, L, "norm", i - 2)
                nc.scalar.activation(nmr[:, cols], mv[:, cols, 1], ACT.Sqrt, bias=eps_c[:, :],
                                     scale=1.0 / ST ** 2).then_inc(ls["std"], 1)
            if 0 <= i - 8 < T:
                t = i - 8
                wait_layer(nc.scalar, L, "inv", 2 * (t // 4) + 2)
                if t >= 2:
                    wait_layer(nc.scalar, L, "h_lo", t - 1)
                nc.scalar.activation(HSC[:, t % 2, :], X[:, t, :], ACT.Relu, bias=nmr[:, t:t + 1],
                                     scale=rstd[:, t:t + 1]).then_inc(ls["h_pre"], 1)
                wait_layer(nc.scalar, L, "h_pre", t + 1)
                nc.scalar.activation(hn[:, t, 0, :], HSC[:, t % 2, :], ACT.Copy).then_inc(ls["h_hi"], 1)
            if i >= 16 and (i - 14) % 4 == 2 and i - 14 < T:
                turn_copy(L, ht, (i - 14) // 2)

        def turn_at(i):
            return (i - 13) // 2 if i >= 13 and i % 2 and (i - 13) // 2 < T // 2 else None

        def turn_tensor(L, hn, q):
            if q >= 2:
                wait_layer(nc.tensor, L, "turn_a" if q % 2 else "turn_v", q // 2)
            for i in range(2):
                t = 2 * q + i
                wait_layer(nc.tensor, L, "h_hi", t + 1)
                wait_layer(nc.tensor, L, "h_lo", t + 1)
                for s in range(2):
                    for k in range(K):
                        mm = nc.tensor.transpose(
                            PS16[4 + q % 2][:, (s * K + k) * 256 + i * P:(s * K + k) * 256 + (i + 1) * P],
                            hn[:, t, s, k * P:(k + 1) * P], ident[:, :])
            mm.then_inc(ls["turned"], 1)

        def turn_copy(L, ht, q):
            dst = ht.rearrange("p s k n -> p (s k) n")[:, :, q * 256:(q + 1) * 256]
            src = PS16[4 + q % 2].rearrange("p (s n) -> p s n", s=4)
            if q % 2:
                wait_layer(nc.scalar, L, "turned", q + 1)
                nc.scalar.activation(dst, src, ACT.Copy).then_inc(ls["turn_a"], 1)
            else:
                wait_layer(nc.vector, L, "turned", q + 1)
                nc.vector.tensor_copy(dst, src).then_inc(ls["turn_v"], 1)

        def turned(eng, L):
            wait_layer(eng, L, "turn_a", T // 4)
            wait_layer(eng, L, "turn_v", T // 4)

        def sum_part(adj, n, t0, t1, mm_sem):
            c, k = n // K, n % K
            for t in range(t0, t1):
                for s in range(2):
                    mm = nc.tensor.matmul(PS[:, n, :], HN[:, t, s, k * P:(k + 1) * P],
                                          adj[:, t, c * CH:(c + 1) * CH], start=(t == 0 and s == 0),
                                          stop=(t == T - 1 and s == 1))
            if t1 == T:
                mm.then_inc(mm_sem, 1)

        def first_sums(adj, L, mm_sem):
            for n in (2, 3, 0, 1):
                if n == 0 and L > 1:
                    nc.tensor.wait_ge(d_v[L - 1], T)
                    nc.tensor.wait_ge(d_sf[L - 1], T)
                sum_part(adj, n, 0, 4, mm_sem)
                if n % 2:
                    turn_tensor(L, HN, 2 if n == 3 else 3)
            for n in range(4):
                sum_part(adj, n, 4, TH, mm_sem)
                turn_tensor(L, HN, 4 + n)
            for n in range(4):
                sum_part(adj, n, TH, T, mm_sem)
            turned(nc.tensor, L)
            for n in range(4, K * NC):
                sum_part(adj, n, 0, T, mm_sem)

        def sum_scalar(n, mm_sem, hi_sem, base):
            c, k = n // K, n % K
            nc.scalar.wait_ge(mm_sem, base + n + 1)
            nc.scalar.activation(QT[:, 0, k, c * CH:(c + 1) * CH], PS[:, n, :], ACT.Copy, scale=1.0 / ST)\
                .then_inc(hi_sem, 1)

        def sum_vector(n, mm_sem, hi_sem, lo_sem, base):
            c, k = n // K, n % K
            nc.vector.wait_ge(hi_sem, base + n + 1)
            nc.vector.scalar_tensor_tensor(QT[:, 1, k, c * CH:(c + 1) * CH], PS[:, n, :], 1.0 / ST,
                                           QT[:, 0, k, c * CH:(c + 1) * CH], ALU.mult, ALU.subtract)\
                .then_inc(lo_sem, 1)

        def rows_tensor(dst, src, wt, t, width, bias):
            for k in range(K):
                for a, b in PARTS:
                    mm = nc.tensor.matmul(dst, src[:, a, k, t * P:(t + 1) * P], wt[:, b, k, 0:width],
                                          start=(k == 0 and a == b == 0),
                                          stop=(not bias and k == K - 1 and a == 1))
            if bias:
                mm = nc.tensor.matmul(dst, ones[:, :], brow[:, 0:width], start=False, stop=True)
            return mm

        @block.tensor
        def _(pe):
            t_ = nc.tensor
            pe.wait_ge(w0_in, 32)
            pe.wait_ge(asel_in, 16 * 2 * H)
            pe.wait_ge(b0_in, 32)
            for dk in range(K):
                for k in range(K):
                    t_.matmul(PS[:, 7, dk * 2 * H:(dk + 1) * 2 * H], STG0[:, 1, k, dk * P:(dk + 1) * P],
                              a_sel[:, k, :], start=(k == 0), stop=(k == K - 1))
            for k in range(K):
                mm = t_.matmul(PS[0:1, 7, 4 * H:6 * H], b_col[:, k:k + 1], a_sel[:, k, :],
                               start=(k == 0), stop=(k == K - 1))
            mm.then_inc(fold0, 1)
            pe.wait_ge(consts, 4)
            for q in range(T // 2):
                turn_tensor(0, HN0, q)
                m, dk = (q - 3) // K, (q - 3) % K
                if 0 <= m < 2:
                    if m == dk == 0:
                        pe.wait_ge(w1_in, 16 * 6)
                    for k in range(K):
                        mm = t_.matmul(PS[:, m, dk * D:(dk + 1) * D], STG1[:, m, k, dk * P:(dk + 1) * P],
                                       STG1[:, 2 + m, k, :], start=(k == 0), stop=(k == K - 1))
                    if dk == K - 1:
                        mm.then_inc(wc_mm, 1)
            pe.wait_ge(b1_in, 16 * 2)
            for m in range(2):
                for k in range(K):
                    mm = t_.matmul(PS[0:1, 2, 0:D], b_col[:, (m + 1) * K + k:(m + 1) * K + k + 1],
                                   STG1[:, 2 + m, k, :], start=(m == k == 0), stop=(m == 1 and k == K - 1))
            mm.then_inc(b1_mm, 1)
            def count_tensor(t):
                pe.wait_ge(at_in[t // 2], 32)
                for c in range(NC):
                    if t >= 1:
                        pe.wait_ge(cum_cp, 2 * (t - 1) + c // 2 + 1)
                    mm = t_.matmul(PS[:, c, :], tri[:, :], AT[:, t, c * CH:(c + 1) * CH], start=True, stop=(t == 0))
                    if t >= 1:
                        mm = t_.matmul(PS[:, c, :], last_row[:, :], CS[:, (t - 1) % 2, c * CH:(c + 1) * CH],
                                       start=False, stop=True)
                    mm.then_inc(cum_mm, 1)

            turned(pe, 0)
            pe.wait_ge(w0_hi, 2)
            pe.wait_ge(w0_lo, 2)
            pe.wait_ge(brow_hi, 2)
            pe.wait_ge(brow_lo, 2)
            pe.wait_ge(wc_hi, 4)
            pe.wait_ge(wc_lo, 4)
            pe.wait_ge(b1_lo, 1)
            for t in range(T):
                if t >= 2:
                    pe.wait_ge(feat_out, 2 * (t - 1))
                rows_tensor(PS[:, 6 + t % 2, 0:DC], HT0, W0, t, DC, True).then_inc(feat, 1)
                if t % 2:
                    count_tensor(t // 2)
            count_tensor(TH)
            for c in range(NC):
                if c == 0:
                    pe.wait_ge(feat_out, 2 * T)
                if c >= 2:
                    pe.wait_ge(srow_out, c - 1)
                for k in range(K):
                    for a, b in PARTS:
                        t_.matmul(PS[0:H, 6 + c % 2, :], W0[:, a, k, D:D + H], HT0[:, b, k, c * CH:(c + 1) * CH],
                                  start=(k == 0 and a == b == 0), stop=False)
                t_.matmul(PS[0:H, 6 + c % 2, :], brow[:, D:D + H],
                          ones[:, :].unsqueeze(1).to_broadcast([P, CH // P, P]),
                          start=False, stop=True).then_inc(srow_mm, 1)
            for t in range(TH + 1, T):
                count_tensor(t)
            for c in range(NC):
                pe.wait_ge(cum_cp, 2 * T)
                t_.matmul(PS[:, c, :], last_row[:, :], CS[:, (T - 1) % 2, c * CH:(c + 1) * CH],
                          start=True, stop=True).then_inc(degb_mm, 1)
            pe.wait_ge(degb_cp, NC)
            for t in range(T):
                mm = t_.matmul(PS[:, 4, t:t + 1], degb[:, t * P:(t + 1) * P], share[:, 0:1], start=True, stop=True)
            mm.then_inc(deg_mm, 1)
            pe.wait_ge(ft_hi, T)
            pe.wait_ge(ft_lo, T)


            def head_tensor(h, first):
                for half in range(2):
                    if first and half == 1:
                        pe.wait_ge(deg_cp, 1)
                    if not first:
                        pe.wait_ge(t_sum, h * 2 + half - 1)
                    for t in range(T):
                        ft = h * (T * FTW) + t * FTW
                        for i in range(TH):
                            t_.matmul(PS[:, 4 * half + i // 2, i % 2 * 256 + 4 * E:i % 2 * 256 + 6 * E],
                                      AT[:, t, half * HALF + i * P:half * HALF + (i + 1) * P],
                                      FTF[:, bass.ds(ft + 2 * E, 2 * E)],
                                      start=(t == 0 and i % 2 == 0), stop=False, skip_group_check=True)
                        pe.wait_ge(m_ready, h * (2 * T) + half * T + t + 1)
                        for i in range(TH):
                            mm = t_.matmul(PS[:, 4 * half + i // 2, i % 2 * 256:i % 2 * 256 + 4 * E],
                                           MS[:, t % NM, i * P:(i + 1) * P], FTF[:, bass.ds(ft, FTW)],
                                           start=False, stop=(t == T - 1), skip_group_check=True)
                        mm.then_inc(m_used, 1)

            head_tensor(0, True)
            with pe.Fori(1, H) as h:
                head_tensor(h, False)

            pe.wait_ge(t_sum, 2 * H)

            def fold_gate(g, bank, slot):
                for dk in range(K):
                    n = 0
                    for m in range(2):
                        for k in range(K):
                            mm = t_.matmul(PS[:, bank, dk * D:(dk + 1) * D], STG3[:, 4 + m, k, dk * P:(dk + 1) * P],
                                           STG3[:, slot + m, k, :], start=(n == 0), stop=(n == 3))
                            n += 1
                for k2 in range(K):
                    n = 0
                    for m in range(2):
                        for k in range(K):
                            mm = t_.matmul(PS[:, 6, g * K + k2:g * K + k2 + 1],
                                           STG3[:, slot + m, k, k2 * P:(k2 + 1) * P],
                                           b_col[:, m * K + k:m * K + k + 1], start=(n == 0), stop=(n == 3))
                            n += 1
                mm.then_inc(v_mm, 1)

            for L in (1, 2):
                if L == 1:
                    for q in range(2):
                        turn_tensor(1, HN, q)
                first_sums(AT if L == 1 else KT, L, q_mm[L])
                if L == 1:
                    pe.wait_ge(b1_hi, 1)
                    pe.wait_ge(b1_lo, 2)
                else:
                    pe.wait_ge(b2_hi, 1)
                    pe.wait_ge(b2_lo, 1)
                pe.wait_ge(q_lo[L], 7)
                if L == 1:
                    pe.wait_ge(w3_in[0], 16 * 12)
                    pe.wait_ge(w3_in[1], 16 * 4)
                    fold_gate(0, 2, 0)
                    fold_gate(1, 3, 2)
                else:
                    pe.wait_ge(w3_in[2], 16 * 3)
                    fold_gate(2, 2, 0)
                for t in range(T):
                    pe.wait_ge(q_lo[L], K * NC)
                    if t >= 3:
                        pe.wait_ge(d_v[L], t - 2)
                        pe.wait_ge(d_sf[L], t - 2)
                    rows_tensor(PS[:, BANK[t % 3], 0:D], HT, W1S if L == 1 else W2S, t, D, True)
                    rows_tensor(PS[:, BANK[t % 3], D:2 * D], QT, W1Q if L == 1 else W2Q, t, D, False)\
                        .then_inc(d_mm[L], 1)
                    if turn_at(t) is not None:
                        turn_tensor(L + 1, HN, turn_at(t))
                pe.wait_ge(w3_hi, 6 if L == 1 else 8)
                pe.wait_ge(w3_lo, 6 if L == 1 else 8)
                pe.wait_ge(v_hi, L)


            def gate_tensor(bank, gate, k2, c, state, cols):
                o = slice(k2 * P, (k2 + 1) * P)
                for k in range(K):
                    for a, b in PARTS:
                        t_.matmul(PS[:, bank, :], WQG[gate][:, a, k, o], QT[:, b, k, c * CH:(c + 1) * CH],
                                  start=(k == 0 and a == b == 0), stop=False)
                for k in range(K):
                    for a, b in PARTS:
                        mm = t_.matmul(PS[:, bank, :], WSG[gate][:, a, k, o], state[:, b, k, cols],
                                       start=False, stop=(k == K - 1 and a == 1))
                return mm

            def step_sums(step):
                def part(n, t0, t1):
                    sum_part(AT, n, t0, t1, q_mm[0])

                for n in range(3):
                    pe.wait_ge(rz_act, step * (4 * NC) - K * 2 + n + 1)
                    pe.wait_ge(back_cp, step * (2 * NC) - 4)
                    part(n, 0, T // 2)
                back(step - 1, NC - 2)
                pe.wait_ge(rz_act, step * (4 * NC))
                part(3, 0, T // 2)
                for n in range(4):
                    pe.wait_ge(back_cp, step * (2 * NC) - 2)
                    part(n, T // 2, T - 4)
                back(step - 1, NC - 1)
                for n in range(4):
                    pe.wait_ge(back_cp, step * (2 * NC))
                    part(n, T - 4, T)
                for n in range(4, K * NC):
                    part(n, 0, T)

            def back(step, c):
                for q in range(2):
                    if c == 0:
                        pe.wait_ge(q_lo[0], step * (K * NC) + 6 + q + 1)
                    else:
                        pe.wait_ge(back_cp, step * (2 * NC) + 2 * (c - 1) + q + 1)
                    pe.wait_ge(new_hi, step * (K * NC) + K * (c + 1))
                    pe.wait_ge(new_lo, step * (K * NC) + K * (c + 1))
                    for i in range(2):
                        t = 4 * c + 2 * q + i
                        for s in range(2):
                            for k in range(K):
                                mm = t_.transpose(
                                    PS16[6 + q][:, i * 2 * D + s * D + k * P:i * 2 * D + s * D + (k + 1) * P],
                                    HT[:, s, k, t * P:(t + 1) * P], ident[:, :])
                    mm.then_inc(back_mm, 1)

            def step_gates(step, last):
                def rz(c):
                    pe.wait_ge(q_lo[0], (step + 1) * (K * NC) if c == NC - 1 else step * (K * NC) + K * (c + 1))
                    for gate in range(2):
                        for k2 in range(K):
                            bank = gate * K + k2
                            if c == 0:
                                pe.wait_ge(q_lo[0], step * (K * NC) + bank + 1)
                            else:
                                pe.wait_ge(rz_act, step * (4 * NC) + 4 * (c - 1) + bank + 1)
                            gate_tensor(bank, gate, k2, c, HT, slice(c * CH, (c + 1) * CH)).then_inc(rz_mm, 1)

                def hg(c):
                    pe.wait_ge(rs_hi, step * (K * NC) + K * (c + 1))
                    pe.wait_ge(rs_lo, step * (K * NC) + K * (c + 1))
                    for k2 in range(K):
                        if c == 0:
                            pe.wait_ge(q_lo[0], step * (K * NC) + 4 + k2 + 1)
                        else:
                            pe.wait_ge(h_act, step * (K * NC) + K * (c - 1) + k2 + 1)
                        gate_tensor(4 + k2, 2, k2, c, RSB[:, c % 2], slice(0, CH)).then_inc(h_mm, 1)

                rz(0)
                rz(1)
                hg(0)
                rz(2)
                hg(1)
                if not last:
                    back(step, 0)
                rz(3)
                hg(2)
                if not last:
                    back(step, 1)
                hg(3)

            first_sums(AT, 3, q_mm[0])
            with pe.Fori(0, STEPS - 1) as step:
                step_gates(step, False)
                step_sums(step + 1)
            step_gates(STEPS - 1, True)

            pe.wait_ge(rz_act, STEPS * 4 * NC)
            pe.wait_ge(h_act, STEPS * K * NC)
            for n in range(K * NC):
                c, k2 = n // K, n % K
                pe.wait_ge(new_hi, ((STEPS - 1) * NC + c + 1) * K)
                pe.wait_ge(new_lo, ((STEPS - 1) * NC + c + 1) * K)
                o = slice(k2 * P, (k2 + 1) * P)
                for k in range(K):
                    for a, b in PARTS:
                        mm = t_.matmul(PS[:, n, :], WO1[:, a, k, o], HT[:, b, k, c * CH:(c + 1) * CH],
                                       start=(k == 0 and a == b == 0), stop=(k == K - 1 and a == 1))
                mm.then_inc(o1_mm, 1)
            pe.wait_ge(bo_hi, 1)
            pe.wait_ge(bo_lo, 1)
            for t in range(T):
                pe.wait_ge(o1_lo, K * (t // (CH // P) + 1))
                if t >= 2:
                    pe.wait_ge(o2_x, t - 1)
                rows_tensor(PS[:, t % 2, 0:D], QT, WO2, t, D, True).then_inc(o2_mm, 1)

        @block.scalar
        def _(act):
            a_ = nc.scalar
            act.wait_ge(pool_c, 5)
            act.wait_ge(brow_zero, 1)
            for i in range(LN_STEPS):
                norm_scalar(0, HN0, HT0, i)
                if i == W0_AT:
                    act.wait_ge(w0_in, 32)
                    act.wait_ge(b0_in, 32)
                    a_.activation(W0[:, 0, :, 0:D], STG0[:, 0], ACT.Copy, scale=WS).then_inc(w0_hi, 1)
                    a_.activation(brow[0:1, 0:D], b_row[0:1, 0:D], ACT.Copy, scale=PR).then_inc(brow_hi, 1)
            act.wait_ge(fold0, 1)
            a_.activation(W0[:, 0, :, D:DC], PS[:, 7, 0:4 * H].rearrange("p (k c) -> p k c", k=K), ACT.Copy,
                          scale=WS).then_inc(w0_hi, 1)
            a_.activation(brow[0:1, D:DC], PS[0:1, 7, 4 * H:6 * H], ACT.Copy, scale=PR).then_inc(brow_hi, 1)

            def count_scalar(t, halves=(0, 1)):
                for c in halves:
                    act.wait_ge(cum_mm, NC * t + 2 * c + 2)
                    if t >= 2:
                        act.wait_ge(kept, 2 * (t - 2) + c + 1)
                    a_.activation(CS[:, t % 2, c * HALF:(c + 1) * HALF].rearrange("p (b n) -> p b n", b=2),
                                  PS[:, 2 * c:2 * c + 2, :], ACT.Copy).then_inc(cum_cp, 1)

            act.wait_ge(wc_mm, 2)
            for m, wt in ((0, W1S), (1, W1Q)):
                a_.activation(wt[:, 0], PS[:, m, :].rearrange("p (k d) -> p k d", k=K), ACT.Copy,
                              scale=(WS, WQ)[m]).then_inc(wc_hi, 1)
            for m, wt in ((0, W2S), (1, W2Q)):
                a_.activation(wt[:, 0], STG1[:, 4 + m], ACT.Copy, scale=(WS, WQ)[m]).then_inc(wc_hi, 1)

            for t in range(T):
                act.wait_ge(feat, t + 1)
                if t == 0:
                    act.wait_ge(consts, 4)
                a_.activation(HF[:, t, :, 0:DH], PS[:, 6 + t % 2, 0:D].rearrange("p (h c) -> p h c", h=H),
                              ACT.Copy, scale=1.0 / PR).then_inc(feat_out, 1)
                a_.activation(sv[:, t, :], PS[:, 6 + t % 2, D:DC], ACT.Copy, scale=1.0 / PR).then_inc(feat_out, 1)
                if t % 2:
                    count_scalar(t // 2)
            count_scalar(TH)
            for c in range(NC):
                act.wait_ge(srow_mm, c + 1)
                a_.activation(SROW[0:H, c * CH:(c + 1) * CH], PS[0:H, 6 + c % 2, :], ACT.Copy, scale=1.0 / PR)\
                    .then_inc(srow_out, 1)
            act.wait_ge(b1_lo, 1)
            a_.activation(brow[0:1, 0:D], b_row[0:1, 0:D], ACT.Copy, scale=PR).then_inc(b1_hi, 1)
            act.wait_ge(tabs_d, 1)
            a_.activation(E1, SCR, ACT.Exp, bias=up_c[:, :]).then_inc(tabs_e, 1)
            a_.activation(E2, SCR, ACT.Exp, bias=up_c[:, :], scale=0.2).then_inc(tabs_e, 1)
            count_scalar(TH + 1)
            act.wait_ge(tabs, 5)
            a_.activation(CA, CA, ACT.Exp).then_inc(tabs_e, 1)
            a_.activation(CB, CB, ACT.Exp).then_inc(tabs_e, 1)
            for t in range(T):
                act.wait_ge(g_done, 2 * t + 2)
                a_.activation(FT[:, :, t, :, 0, :], GR[:, t % 2], ACT.Copy).then_inc(ft_hi, 1)
                if t >= 4:
                    count_scalar(TH + t // 2, (t % 2,))
            for c in range(NC):
                act.wait_ge(degb_mm, c + 1)
                a_.activation(degb[:, c * CH:(c + 1) * CH], PS[:, c, :], ACT.Copy).then_inc(degb_cp, 1)
            act.wait_ge(kept, 2 * T)
            act.wait_ge(ft_lo, T)

            def low_out(h, half):
                act.wait_ge(m_used, h * (2 * T) + (half + 1) * T)
                if not (isinstance(h, int) and h == 0 and half == 0):
                    act.wait_ge(t_sum, h * 2 + half)
                a_.activation(TMP, PS[:, 4 * half:4 * half + 4, :].rearrange("p b (i n) -> p (b i) n", i=2)
                              [:, :, 0:6 * E].rearrange("p t (g s c) -> p t g s c", g=3, s=2)[:, :, :, 1, :],
                              ACT.Copy).then_inc(lo_out, 1)

            def elu_exp(h, half):
                act.wait_ge(neg_ready, h * 2 + half + 1)
                if not (isinstance(h, int) and h == 0 and half == 0):
                    act.wait_ge(x_heads, h * 2 + half)
                a_.activation(TE, TN, ACT.Exp).then_inc(exp_ready, 1)

            def head_scalar(h, first):
                def scores(half):
                    a_.activation(bigs[:, half, :], BIGS[:, bass.ds(h, 1), :].rearrange("p a t -> p (a t)"),
                                  ACT.Copy).then_inc(bigs_in, 1)

                scores(0)
                for half in range(2):
                    act.wait_ge(bigs_in, h * 2 + half + 1)
                    act.wait_ge(sbc_in[half], h * 16 + 16)
                    n = 0
                    for t in range(T):
                        if t in ALONE:
                            continue
                        if n == 2 and not (first and half == 0):
                            low_out(h - (half == 0), 1 - half)
                        if n == 9 and half == 0:
                            scores(1)
                        if n == 11 and not (first and half == 0):
                            elu_exp(h - (half == 0), 1 - half)
                        f = half * NYH + n - NY
                        if f >= 0:
                            act.wait_ge(m_ready, h * (2 * T) + f // NYH * T + STARTED[f % NYH] + 1)
                        elif not first:
                            act.wait_ge(m_ready, h * (2 * T) + STARTED[NYH + f] + 1 - T)
                        a_.activation(YS[:, n % NY, :], SBC[:, half, :], ACT.Relu, scale=BIG,
                                      bias=bigs[:, half, t:t + 1])\
                            .then_inc(y_ready, 1)
                        n += 1

            head_scalar(0, True)
            with act.Fori(1, H) as h:
                head_scalar(h, False)
            low_out(H - 1, 1)
            for i in range(LN_BEGUN):
                norm_scalar(1, HN, HT, i)
            elu_exp(H - 1, 1)
            def state_high(n, m, wt):
                a_.activation(wt[:, 0], STG3[:, m], ACT.Copy, scale=WS).then_inc(w3_hi, 1)

            def fold_high(g, bank):
                a_.activation(WQG[g][:, 0], PS[:, bank, :].rearrange("p (k d) -> p k d", k=K), ACT.Copy, scale=WQ)\
                    .then_inc(w3_hi, 1)

            for L in (1, 2):
                if L == 1:
                    for i in range(LN_BEGUN, LN_STEPS):
                        norm_scalar(1, HN, HT, i)
                if L == 1:
                    act.wait_ge(w3_in[0], 16 * 12)
                    for m, wt in enumerate(WSG + [WO1]):
                        state_high(m, m, wt)
                else:
                    act.wait_ge(w3_in[2], 16 * 3)
                    state_high(6, 2, WO2)
                for n in range(K * NC):
                    sum_scalar(n, q_mm[L], q_hi[L], 0)
                for t in range(LN_STEPS):
                    if t < T:
                        act.wait_ge(d_mm[L], t + 1)
                        if t >= 2:
                            act.wait_ge(d_v[1] if L == 1 else d_u[2], t - 1)
                        if L == 2:
                            a_.activation(SF01[:, t % 2, :], PS[:, BANK[t % 3], 0:D], ACT.Copy, scale=0.01 / PR)\
                                .then_inc(d_xi, 1)
                            a_.activation(SF[:, t % 2, :], PS[:, BANK[t % 3], 0:D], ACT.Relu, scale=0.99 / PR)\
                                .then_inc(d_sf[2], 1)
                        else:
                            a_.activation(SF[:, t % 2, :], PS[:, BANK[t % 3], 0:D], ACT.Copy, scale=1.0 / PR)\
                                .then_inc(d_sf[1], 1)
                    if t == 2 and L == 1:
                        act.wait_ge(v_mm, 2)
                        fold_high(0, 2)
                        fold_high(1, 3)
                        a_.activation(vcol[:, 0:2 * K], PS[:, 6, 0:2 * K], ACT.Copy, scale=PR).then_inc(v_hi, 1)
                    if t == 2 and L == 2:
                        act.wait_ge(v_mm, 3)
                        fold_high(2, 2)
                        a_.activation(vcol[:, 2 * K:3 * K], PS[:, 6, 2 * K:3 * K], ACT.Copy, scale=PR)\
                            .then_inc(v_hi, 1)
                    norm_scalar(L + 1, HN, HT, t)
                if L == 1:
                    act.wait_ge(row_in, 16 * 2)
                    a_.activation(brow[0:1, 0:D], b_row[0:1, 0:D], ACT.Copy, scale=PR).then_inc(b2_hi, 1)
            act.wait_ge(row_in, 16 * 4)
            act.wait_ge(d_mm[2], T)
            a_.activation(brow[0:1, 0:D], b_row[0:1, 0:D], ACT.Copy, scale=PR).then_inc(bo_hi, 1)
            act.wait_ge(x_out, 16)

            def gates_scalar(step, last):
                def gates(c):
                    for gate in range(2):
                        for k2 in range(K):
                            n = 4 * c + gate * K + k2
                            act.wait_ge(rz_deg, step * (4 * NC) + n + 1)
                            if gate == 0:
                                dst = RG[:, k2, :]
                                if c >= 1:
                                    act.wait_ge(rs_lo, step * (K * NC) + K * (c - 1) + k2 + 1)
                            else:
                                dst = ZR[:, c % 2, k2, :]
                                if c >= 2:
                                    act.wait_ge(new_f, step * (K * NC) + K * (c - 2) + k2 + 1)
                            a_.activation(dst, PS[:, gate * K + k2, :], ACT.Sigmoid, scale=1.0 / PR,
                                          bias=b_col[:, (4 + gate) * K + k2:(4 + gate) * K + k2 + 1])\
                                .then_inc(rz_act, 1)

                def rs_high(c):
                    for k2 in range(K):
                        act.wait_ge(rs_f, step * (K * NC) + K * c + k2 + 1)
                        a_.activation(RSB[:, c % 2, 0, k2, :], RG[:, k2, :], ACT.Copy).then_inc(rs_hi, 1)

                def tanh(c):
                    for k2 in range(K):
                        n = K * c + k2
                        act.wait_ge(h_deg, step * (K * NC) + n + 1)
                        if c >= 1:
                            act.wait_ge(new_lo, step * (K * NC) + n - 1)
                        a_.activation(HG[:, k2, :], PS[:, 4 + k2, :], ACT.Tanh, scale=1.0 / PR,
                                      bias=b_col[:, 6 * K + k2:6 * K + k2 + 1]).then_inc(h_act, 1)

                def new_high(c):
                    for k2 in range(K):
                        n = K * c + k2
                        act.wait_ge(new_f, step * (K * NC) + n + 1)
                        a_.activation(HT[:, 0, k2, c * CH:(c + 1) * CH], HG[:, k2, :], ACT.Copy)\
                            .then_inc(new_hi, 1)

                def back_out(c):
                    for q in range(2):
                        act.wait_ge(back_mm, step * (2 * NC) + 2 * c + q + 1)
                        t = 4 * c + 2 * q
                        a_.activation(HN[:, t:t + 2].rearrange("p t s d -> p (t s d)"), PS16[6 + q], ACT.Copy)\
                            .then_inc(back_cp, 1)

                gates(0)
                rs_high(0)
                gates(1)
                rs_high(1)
                tanh(0)
                new_high(0)
                gates(2)
                rs_high(2)
                tanh(1)
                new_high(1)
                if not last:
                    back_out(0)
                gates(3)
                rs_high(3)
                tanh(2)
                new_high(2)
                if not last:
                    back_out(1)
                tanh(3)
                if not last:
                    back_out(2)
                new_high(3)
                if not last:
                    back_out(3)

            def sums_scalar(step):
                for n in range(K * NC):
                    sum_scalar(n, q_mm[0], q_hi[0], step * (K * NC))

            sums_scalar(0)
            with act.Fori(0, STEPS - 1) as step:
                gates_scalar(step, False)
                sums_scalar(step + 1)
            gates_scalar(STEPS - 1, True)

            act.wait_ge(new_lo, STEPS * K * NC)
            for n in range(K * NC):
                c, k2 = n // K, n % K
                act.wait_ge(o1_mm, n + 1)
                if n >= 2:
                    act.wait_ge(o1_lo, n - 1)
                a_.activation(HG[:, n % 2, :], PS[:, n, :], ACT.Tanh, scale=1.0 / PR,
                              bias=b_col[:, 7 * K + k2:7 * K + k2 + 1]).then_inc(o1_act, 1)
                act.wait_ge(o1_act, n + 1)
                a_.activation(QT[:, 0, k2, c * CH:(c + 1) * CH], HG[:, n % 2, :], ACT.Copy, scale=ST)\
                    .then_inc(o1_hi, 1)


        @block.vector
        def _(dve):
            v = nc.vector

            def sync(sem_, n):
                dve.wait_ge(sem_, n)

            def split_low(lo, src, scale, hi):
                return v.scalar_tensor_tensor(lo, src, scale, hi, ALU.mult, ALU.subtract)

            for i in range(LN_STEPS):
                norm_vector(0, HN0, HT0, i, lambda e, t: e.wait_ge(x_in_s[t // TH], 16))
                if i == W0_AT:
                    sync(w0_in, 32)
                    sync(w0_hi, 1)
                    split_low(W0[:, 1, :, 0:D], STG0[:, 0], WS, W0[:, 0, :, 0:D]).then_inc(w0_lo, 1)
                    sync(brow_hi, 1)
                    split_low(brow[32:33, 0:D], b_row[0:1, 0:D], PR, brow[0:1, 0:D]).then_inc(brow_lo, 1)
            sync(w0_hi, 2)
            sync(brow_hi, 2)
            split_low(W0[:, 1, :, D:DC], PS[:, 7, 0:4 * H].rearrange("p (k c) -> p k c", k=K), WS,
                      W0[:, 0, :, D:DC]).then_inc(w0_lo, 1)
            sync(brow_hi, 2)
            split_low(brow[32:33, D:DC], PS[0:1, 7, 4 * H:6 * H], PR, brow[0:1, D:DC]).then_inc(brow_lo, 1)
            for m, wt in ((0, W1S), (1, W1Q)):
                sync(wc_hi, m + 1)
                split_low(wt[:, 1], PS[:, m, :].rearrange("p (k d) -> p k d", k=K), (WS, WQ)[m], wt[:, 0])\
                    .then_inc(wc_lo, 1)
            for m, wt in ((0, W2S), (1, W2Q)):
                sync(wc_hi, m + 3)
                split_low(wt[:, 1], STG1[:, 4 + m], (WS, WQ)[m], wt[:, 0]).then_inc(wc_lo, 1)
            sync(b1_mm, 1)
            sync(row_in, 16)
            v.tensor_tensor(b_row[0:1, 0:D], b_row[0:1, 0:D], PS[0:1, 2, 0:D], ALU.add).then_inc(b1_lo, 1)

            def keep(t, halves=(0, 1)):
                for c in halves:
                    sync(cum_cp, 2 * t + c + 1)
                    cols = slice(c * HALF, (c + 1) * HALF)
                    v.scalar_tensor_tensor(KT[:, t, cols], CS[:, t % 2, cols], CAP, AT[:, t, cols], ALU.is_le,
                                           ALU.mult, saturate=False).then_inc(kept, 1)

            for t in range(TH):
                keep(t)
            sync(feat_out, 2 * T)
            s_src = sv[:, :, 0:H].rearrange("p t h -> p h t")
            s_dst = sv[:, :, H:2 * H].rearrange("p t h -> p h t")
            v.reduce_max(cm[:, 0, :], s_dst, axis=AX.X).then_inc(cmax_l, 1)
            v.tensor_scalar(BIGS, s_dst, BIG, None, ALU.mult).then_inc(tabs, 1)
            v.tensor_scalar(NEGS, s_dst, -1.0, None, ALU.mult).then_inc(tabs, 1)
            keep(TH)
            sync(cmax, 1)
            top = cm[:, 1, :].unsqueeze(2).to_broadcast([P, H, T])
            v.tensor_tensor(SCR, s_dst, top, ALU.subtract).then_inc(tabs_d, 1)
            v.tensor_tensor(SCM, s_src, top, ALU.add).then_inc(tabs, 1)
            sync(tabs, 3)
            v.scalar_tensor_tensor(CB, SCM, 0.2, SCM, ALU.mult, ALU.max).then_inc(tabs_d, 1)
            sync(tabs_d, 2)
            v.tensor_tensor(CA, SCM, CB, ALU.subtract).then_inc(tabs, 1)
            sync(tabs, 4)
            v.scalar_tensor_tensor(CB, SCM, 0.2, CB, ALU.mult, ALU.subtract).then_inc(tabs, 1)
            keep(TH + 1)
            sync(b1_hi, 1)
            split_low(brow[32:33, 0:D], b_row[0:1, 0:D], PR, brow[0:1, 0:D]).then_inc(b1_lo, 1)
            for t in range(T):
                sync(ft_hi, t + 1)
                v.tensor_tensor(FT[:, :, t, :, 1, :], GR[:, t % 2], FT[:, :, t, :, 0, :], ALU.subtract)\
                    .then_inc(ft_lo, 1)
                if t >= 4:
                    keep(TH + t // 2, (t % 2,))

            def sums(h, half):
                n = h * 2 + half
                dve.wait_ge(lo_out, n + 1)
                if not (isinstance(h, int) and h == 0 and half == 0):
                    dve.wait_ge(t_used, n)
                hi = PS[:, 4 * half:4 * half + 4, :].rearrange("p b (i n) -> p (b i) n", i=2)[:, :, 0:6 * E]\
                    .rearrange("p t (g s c) -> p t g s c", g=3, s=2)[:, :, :, 0, :]
                v.tensor_tensor(TSUM, hi, TMP, ALU.add).then_inc(t_sum, 1)

            def shares(h, half):
                dve.wait_ge(mixed, h * 2 + half + 1)
                v.reciprocal(REC[:, :], TA[:, :, DH]).then_inc(share_out, 1)

            def head_vector(h, first):
                for half in range(2):
                    dve.wait_ge(sbc_in[half], h * 16 + 16)
                    n = 0
                    for t in range(T):
                        if first and half == 0 and t == 4:
                            sync(deg_mm, 1)
                            v.tensor_scalar(deg[:, 0, :], PS[:, 4, 0:T], 1.0, None, ALU.mult).then_inc(deg_cp, 1)
                        if t == 4 and not (first and half == 0):
                            sums(h - (half == 0), 1 - half)
                        if t == 9 and not (first and half == 0):
                            shares(h - (half == 0), 1 - half)
                        if not first or half * T + t >= NM:
                            dve.wait_ge(m_used, h * (2 * T) + half * T + t + 1 - NM)
                        adj = AT[:, t, half * HALF:(half + 1) * HALF]
                        if t in ALONE:
                            v.scalar_tensor_tensor(MS[:, t % NM, :], SBC[:, half, :],
                                                   NEGS[:, bass.ds(h, 1), t:t + 1].rearrange("p a t -> p (a t)"),
                                                   adj, ALU.is_gt, ALU.mult).then_inc(m_ready, 1)
                        else:
                            dve.wait_ge(y_ready, h * (2 * NYH) + half * NYH + n + 1)
                            v.tensor_tensor(MS[:, t % NM, :], YS[:, n % NY, :], adj, ALU.min)\
                                .then_inc(m_ready, 1)
                            n += 1

            head_vector(0, True)
            with dve.Fori(1, H) as h:
                head_vector(h, False)
            def own_row(L):
                def wait(eng, t):
                    if L == 1:
                        eng.wait_ge(x_heads, 2 * H - 1 if t < TH else 2 * H)
                    else:
                        eng.wait_ge(d_x[L - 1], t + 1)
                return wait

            for i in range(LN_BEGUN):
                norm_vector(1, HN, HT, i, own_row(1))
            sums(H - 1, 1)

            def per_source(tab, width):
                return tab[:, H - 1, TH:T].unsqueeze(2).to_broadcast([P, TH, width])

            n = 2 * H
            sync(x_heads, n - 1)
            sync(t_sum, n)
            v.tensor_tensor(TB, TSUM[:, :, 2, :], TSUM[:, :, 1, :], ALU.subtract).then_inc(mix_a, 1)
            v.tensor_tensor(TA, TSUM[:, :, 0, :], per_source(CA, E), ALU.mult).then_inc(mix_a, 1)
            sync(mix_a, 2 * n)
            v.tensor_tensor(TB, TB, per_source(CB, E), ALU.mult).then_inc(t_used, 1)
            sync(t_used, n)
            v.tensor_tensor(TA, TA, TB, ALU.add).then_inc(mixed, 1)
            sync(mixed, n)
            v.reciprocal(REC[:, :], TA[:, :, DH]).then_inc(share_out, 1)
            sync(share_out, n)
            v.tensor_tensor(TV, TA[:, :, 0:DH], REC[:, :].unsqueeze(2).to_broadcast([P, TH, DH]), ALU.mult)\
                .then_inc(divided, 1)
            sync(divided, n)
            v.tensor_scalar(TN, TV, 0.0, None, ALU.min).then_inc(neg_ready, 1)
            v.tensor_scalar(TP, TV, 0.0, -1.0, ALU.max, ALU.add).then_inc(pos_ready, 1)
            last_x = X[:, TH:T, (H - 1) * DH:H * DH]
            sync(pos_ready, n)
            v.tensor_tensor(last_x, last_x, TP, ALU.add).then_inc(pos_added, 1)

            def last_finish():
                sync(pos_added, n)
                sync(exp_ready, n)
                v.tensor_tensor(last_x, last_x, TE, ALU.add).then_inc(x_heads, 1)

            def state_low(n, m, wt):
                sync(w3_hi, n + 1)
                split_low(wt[:, 1], STG3[:, m], WS, wt[:, 0]).then_inc(w3_lo, 1)

            def fold_low(n, g, bank):
                sync(w3_hi, n + 1)
                split_low(WQG[g][:, 1], PS[:, bank, :].rearrange("p (k d) -> p k d", k=K), WQ, WQG[g][:, 0])\
                    .then_inc(w3_lo, 1)

            for L in (1, 2):
                if L == 1:
                    for i in range(LN_BEGUN, LN_STEPS):
                        if i == TH + 1:
                            last_finish()
                        norm_vector(1, HN, HT, i, own_row(1))
                    sync(deg_cp, 1)
                    v.tensor_scalar(deg[:, 1, :], deg[:, 0, :], 1.0, PR, ALU.max, ALU.mult).then_inc(deg_rd, 1)
                    v.tensor_scalar(deg[:, 2, :], deg[:, 0, :], 1.0, None, ALU.min).then_inc(deg_rd, 1)
                    v.tensor_scalar(deg[:, 3, :], deg[:, 0, :], CAP, 1.0, ALU.min, ALU.max).then_inc(deg_rd, 1)
                    sync(deg_rd, 3)
                    v.reciprocal(deg[:, 4, :], deg[:, 1, :]).then_inc(deg_rd, 1)
                    v.reciprocal(deg[:, 5, :], deg[:, 3, :]).then_inc(deg_rd, 1)
                    sync(deg_rd, 5)
                    v.tensor_scalar(deg[:, 5, :], deg[:, 5, :], 1.0 / PR, None, ALU.mult).then_inc(deg_rd, 1)
                    sync(degb_cp, NC)
                if L == 1:
                    for m, wt in enumerate(WSG + [WO1]):
                        state_low(m, m, wt)
                else:
                    state_low(6, 2, WO2)
                    sync(row_in, 16 * 3)
                for n in range(K * NC):
                    sum_vector(n, q_mm[L], q_hi[L], q_lo[L], 0)

                def value(t):
                    sync(d_mm[L], t + 1)
                    sync(d_sf[L], t + 1)
                    if t >= 2:
                        sync(d_x[L], t - 1)
                    v.scalar_tensor_tensor(SV2[:, t % 2, :], PS[:, BANK[t % 3], D:2 * D], deg[:, 3 + L, t:t + 1],
                                           SF[:, t % 2, :] if L == 1 else bn_bc[:, :], ALU.mult, ALU.add)\
                        .then_inc(d_v[L], 1)

                def join(t):
                    sync(d_v[L], t + 1)
                    if L == 1:
                        v.scalar_tensor_tensor(X[:, t, :], SV2[:, t % 2, :], 0.0, X[:, t, :], ALU.max, ALU.add)\
                            .then_inc(d_x[1], 1)
                    else:
                        v.scalar_tensor_tensor(SV2[:, t % 2, :], SV2[:, t % 2, :], 0.01, SV2[:, t % 2, :],
                                               ALU.mult, ALU.max).then_inc(d_lr, 1)
                        sync(d_lr, t + 1)
                        sync(d_u[2], t + 1)
                        v.scalar_tensor_tensor(X[:, t, :], SV2[:, t % 2, :], deg[:, 2, t:t + 1], X[:, t, :],
                                               ALU.mult, ALU.add).then_inc(d_x[2], 1)

                for t in range(LN_STEPS):
                    if t == 3:
                        if L == 1:
                            fold_low(4, 0, 2)
                            fold_low(5, 1, 3)
                        else:
                            fold_low(7, 2, 2)
                    if t < T:
                        value(t)
                    if 1 <= t <= T:
                        join(t - 1)
                    norm_vector(L + 1, HN, HT, t, own_row(L + 1))
                if L == 1:
                    sync(b2_hi, 1)
                    split_low(brow[32:33, 0:D], b_row[0:1, 0:D], PR, brow[0:1, 0:D]).then_inc(b2_lo, 1)

            sync(bo_hi, 1)
            split_low(brow[32:33, 0:D], b_row[0:1, 0:D], PR, brow[0:1, 0:D]).then_inc(bo_lo, 1)
            sync(x_out, 16)

            def sums_of_step(step):
                for n in range(K * NC):
                    sum_vector(n, q_mm[0], q_hi[0], q_lo[0], step * (K * NC))

            def gates_vector(step):
                def old(k2, c):
                    if c >= 3:
                        sync(new_f, step * (K * NC) + K * (c - 3) + k2 + 1)
                    v.tensor_tensor(SG[:, c % 3, k2, :], HT[:, 0, k2, c * CH:(c + 1) * CH],
                                    HT[:, 1, k2, c * CH:(c + 1) * CH], ALU.add).then_inc(st_r, 1)

                def bias(gate, c, mm_sem, mm_base, done):
                    for k2 in range(K):
                        bank = gate * K + k2
                        sync(mm_sem, mm_base + k2 + 1)
                        v.scalar_tensor_tensor(PS[:, bank, :], degb[:, c * CH:(c + 1) * CH],
                                               vcol[:, bank:bank + 1], PS[:, bank, :], ALU.mult, ALU.add)\
                            .then_inc(done, 1)

                def reset(c):
                    bias(0, c, rz_mm, step * (4 * NC) + 4 * c, rz_deg)
                    for k2 in range(K):
                        old(k2, c)
                    for k2 in range(K):
                        sync(st_r, step * (K * NC) + K * c + k2 + 1)
                        sync(rz_act, step * (4 * NC) + 4 * c + k2 + 1)
                        v.tensor_tensor(RG[:, k2, :], RG[:, k2, :], SG[:, c % 3, k2, :], ALU.mult).then_inc(rs_f, 1)
                    bias(1, c, rz_mm, step * (4 * NC) + 4 * c + K, rz_deg)
                    for k2 in range(K):
                        sync(rs_hi, step * (K * NC) + K * c + k2 + 1)
                        v.tensor_tensor(RSB[:, c % 2, 1, k2, :], RG[:, k2, :], RSB[:, c % 2, 0, k2, :],
                                        ALU.subtract).then_inc(rs_lo, 1)

                def update(c):
                    base = step * (K * NC) + K * c
                    bias(2, c, h_mm, base, h_deg)
                    for k2 in range(K):
                        sync(h_act, base + k2 + 1)
                        v.scalar_tensor_tensor(HG[:, k2, :], HG[:, k2, :], ST, SG[:, c % 3, k2, :], ALU.mult,
                                               ALU.subtract).then_inc(up_a, 1)
                    for k2 in range(K):
                        sync(up_a, base + k2 + 1)
                        sync(rz_act, step * (4 * NC) + 4 * c + K + k2 + 1)
                        v.tensor_tensor(HG[:, k2, :], HG[:, k2, :], ZR[:, c % 2, k2, :], ALU.mult)\
                            .then_inc(up_b, 1)
                    for k2 in range(K):
                        sync(up_b, base + k2 + 1)
                        v.tensor_tensor(HG[:, k2, :], HG[:, k2, :], SG[:, c % 3, k2, :], ALU.add).then_inc(new_f, 1)
                    for k2 in range(K):
                        sync(new_hi, base + k2 + 1)
                        v.tensor_tensor(HT[:, 1, k2, c * CH:(c + 1) * CH], HG[:, k2, :],
                                        HT[:, 0, k2, c * CH:(c + 1) * CH], ALU.subtract).then_inc(new_lo, 1)

                reset(0)
                reset(1)
                update(0)
                reset(2)
                update(1)
                reset(3)
                update(2)
                update(3)

            sums_of_step(0)
            with dve.Fori(0, STEPS - 1) as step:
                gates_vector(step)
                sums_of_step(step + 1)
            gates_vector(STEPS - 1)

            for n in range(K * NC):
                c, k2 = n // K, n % K
                sync(o1_hi, n + 1)
                v.scalar_tensor_tensor(QT[:, 1, k2, c * CH:(c + 1) * CH], HG[:, n % 2, :], ST,
                                       QT[:, 0, k2, c * CH:(c + 1) * CH], ALU.mult, ALU.subtract)\
                    .then_inc(o1_lo, 1)
            sync(x_back, 16)
            for t in range(T):
                sync(o2_mm, t + 1)
                v.scalar_tensor_tensor(OB[:, t, :], PS[:, t % 2, 0:D], 1.0 / PR, XF[:, t, :], ALU.mult, ALU.add)\
                    .then_inc(o2_x, 1)


def kernel(x, adj, L0_gnn_W_w, L0_gnn_W_b, L0_gnn_a, L1_gnn_W_self, L1_gnn_b_self, L1_gnn_W_nb, L1_gnn_b_nb,
           L1_gnn_W_comb, L1_gnn_b_comb, L2_gnn_W_nb, L2_gnn_b_nb, L2_gnn_W_line, L2_gnn_b_line, L3_gnn_in_W,
           L3_gnn_in_b, L3_gnn_out_W, L3_gnn_out_b, L3_gnn_r_W, L3_gnn_r_b, L3_gnn_z_W, L3_gnn_z_b, L3_gnn_h_W,
           L3_gnn_h_b, L3_gnn_o1_W, L3_gnn_o1_b, L3_gnn_o2_W, L3_gnn_o2_b):
    import concourse.bacc as bacc
    from concourse.bass_utils import run_bass_kernel_spmd

    arr = np.asarray
    D = x.shape[1]
    data = {
        "x": arr(x), "adj_t": arr(adj).T, "l0_w": arr(L0_gnn_W_w), "l0_wt": arr(L0_gnn_W_w).T,
        "l0_b": arr(L0_gnn_W_b), "l0_a": arr(L0_gnn_a),
        "l1_ws_t": arr(L1_gnn_W_self).T, "l1_wn_t": arr(L1_gnn_W_nb).T,
        "l1_wc1": arr(L1_gnn_W_comb)[:D], "l1_wc2": arr(L1_gnn_W_comb)[D:],
        "l1_bs": arr(L1_gnn_b_self), "l1_bn": arr(L1_gnn_b_nb), "l1_bc": arr(L1_gnn_b_comb),
        "l2_wl_t": arr(L2_gnn_W_line).T, "l2_wn_t": arr(L2_gnn_W_nb).T,
        "l2_bl": arr(L2_gnn_b_line), "l2_bn": arr(L2_gnn_b_nb),
        "l3_in_w": arr(L3_gnn_in_W), "l3_out_w": arr(L3_gnn_out_W),
        "l3_in_b": arr(L3_gnn_in_b), "l3_out_b": arr(L3_gnn_out_b),
        "l3_rb": arr(L3_gnn_r_b), "l3_zb": arr(L3_gnn_z_b), "l3_hb": arr(L3_gnn_h_b),
        "l3_o1_t": arr(L3_gnn_o1_W).T, "l3_o1b": arr(L3_gnn_o1_b),
        "l3_o2_t": arr(L3_gnn_o2_W).T, "l3_o2b": arr(L3_gnn_o2_b),
    }
    for g, wg in (("r", L3_gnn_r_W), ("z", L3_gnn_z_W), ("h", L3_gnn_h_W)):
        for n in range(3):
            data[f"l3_{g}_t{n}"] = arr(wg)[:, n * D:(n + 1) * D].T

    for name in ("l0_b", "l1_bs", "l1_bn", "l3_in_b", "l3_out_b", "l3_rb", "l3_zb", "l3_hb", "l3_o1b"):
        data[name + "_c"] = data[name].reshape(-1, 128).T

    nc = bacc.Bacc("TRN2", target_bir_lowering=False, num_devices=1)
    arrays, aps = {}, {}
    for name, a in data.items():
        a = np.ascontiguousarray(a)
        arrays[f"in_{name}"] = a
        aps[name] = nc.dram_tensor(f"in_{name}", a.shape, mybir.dt.from_np(a.dtype), kind="ExternalInput").ap()
    out = nc.dram_tensor("out", x.shape, mybir.dt.float32, kind="ExternalOutput").ap()
    gnn_stack_kernel(nc, aps.pop("x"), aps.pop("adj_t"), aps, out)
    r = run_bass_kernel_spmd(nc, [arrays], core_ids=[0])
    return r.results[0]["out"]
```
